# Optimizing a Trainium2 kernel written in Bass

```python
import numpy as np
import jax
import jax.numpy as jnp

def _softmax(x, axis=-1):
    return jax.nn.softmax(x, axis=axis)

def _gelu(x):
    return jax.nn.gelu(x, approximate=True)

def _silu(x):
    return jax.nn.silu(x)

def _sigmoid(x):
    return jax.nn.sigmoid(x)

def _layernorm(x, axis=-1, eps=1e-05):
    m = jnp.mean(x, axis=axis, keepdims=True)
    v = jnp.var(x, axis=axis, keepdims=True)
    return (x - m) / jnp.sqrt(v + eps)

def _scatter_add(tgt, idx, src, axis=0):
    return tgt.at[idx].add(src)

def _segment_sum(src, seg, n):
    return jax.ops.segment_sum(src, seg, n)
kernel_name = 'mk_seq_postln_d1_jaxref_r8_546702'

def setup_inputs(seed: int=0):
    np.random.seed(seed)
    _w = jnp.asarray

    def _L0_attn_setup():
        import jax, jax.numpy as jnp
        import numpy as np
        B, T, E, H, W = (2, 256, 128, 16, 128)
        D = E // H
        SCALE = 1.0 / float(np.sqrt(D))

        def _sliding_window_mask(t, window):
            i = jnp.arange(t)[:, None]
            j = jnp.arange(t)[None, :]
            return (j <= i) & (j >= i - window + 1)
        key = jax.random.key(seed)
        k1, k2, k3 = jax.random.split(key, 3)
        x = jax.random.normal(k1, (B, T, E), dtype=jnp.float32)
        w_qkv = jax.random.normal(k2, (3 * E, E), dtype=jnp.float32) * 0.02
        w_out = jax.random.normal(k3, (E, E), dtype=jnp.float32) * 0.02
        return {'x': x, 'w_qkv': w_qkv, 'w_out': w_out}
    _L0_attn_in = _L0_attn_setup()

    def _L0_ffn_setup():
        import jax, jax.numpy as jnp
        import numpy as np
        D, H, E, K = (128, 128, 8, 2)

        def _moe(x, router_w, w_in, b_in, w_out, b_out):
            B, S, Dm = x.shape
            T = B * S
            x2 = x.reshape(T, Dm)
            logits = x2 @ router_w
            probs = jax.nn.softmax(logits, axis=-1)
            top_p, top_e = jax.lax.top_k(probs, K)
            flat_e = top_e.reshape(-1)
            flat_p = top_p.reshape(-1)
            tok = jnp.repeat(jnp.arange(T), K)
            order = jnp.argsort(flat_e)
            se, sp, st = (flat_e[order], flat_p[order], tok[order])
            xd = x2[st]
            N = xd.shape[0]
            h = jnp.zeros((N, H), x.dtype)
            for e in range(E):
                m = (se == e)[:, None]
                h = h + jnp.where(m, jax.nn.gelu(xd @ w_in[e] + b_in[e]), 0.0)
            y = jnp.zeros((N, Dm), x.dtype)
            for e in range(E):
                m = (se == e)[:, None]
                y = y + jnp.where(m, h @ w_out[e] + b_out[e], 0.0)
            y = y * sp[:, None]
            out = jnp.zeros((T, Dm), x.dtype).at[st].add(y)
            return out.reshape(B, S, Dm)
        key = jax.random.key(seed)
        ks = jax.random.split(key, 5)
        s = lambda k, shape, scale: jax.random.normal(k, shape, dtype=jnp.float32) * scale
        return {'input_batch': s(ks[0], (2, 64, D), 1.0), 'router_w': s(ks[1], (D, E), D ** (-0.5)), 'w_in': s(ks[2], (E, D, H), D ** (-0.5)), 'b_in': jnp.zeros((E, H), jnp.float32), 'w_out': s(ks[3], (E, H, D), H ** (-0.5)), 'b_out': jnp.zeros((E, D), jnp.float32)}
    _L0_ffn_in = _L0_ffn_setup()
    _d = {'L0_attn_x': _L0_attn_in['x'], 'L0_attn_w_qkv': _L0_attn_in['w_qkv'], 'L0_attn_w_out': _L0_attn_in['w_out'], 'L0_ffn_router_w': _L0_ffn_in['router_w'], 'L0_ffn_w_in': _L0_ffn_in['w_in'], 'L0_ffn_b_in': _L0_ffn_in['b_in'], 'L0_ffn_w_out': _L0_ffn_in['w_out'], 'L0_ffn_b_out': _L0_ffn_in['b_out']}
    _x0 = _d['L0_attn_x']
    _d['L0_attn_x'] = jax.random.normal(jax.random.fold_in(jax.random.key(seed), 1), (8, 256, 128), dtype=_x0.dtype)
    del _x0
    return _d

def reference(L0_attn_x, L0_attn_w_qkv, L0_attn_w_out, L0_ffn_router_w, L0_ffn_w_in, L0_ffn_b_in, L0_ffn_w_out, L0_ffn_b_out):

    def _L0_attn_ref(x, w_qkv, w_out):
        import jax, jax.numpy as jnp
        import numpy as np
        B, T, E, H, W = (2, 256, 128, 16, 128)
        D = E // H
        SCALE = 1.0 / float(np.sqrt(D))

        def _sliding_window_mask(t, window):
            i = jnp.arange(t)[:, None]
            j = jnp.arange(t)[None, :]
            return (j <= i) & (j >= i - window + 1)
        b, t, e = x.shape
        qkv = x @ w_qkv.T
        q, k, v = jnp.split(qkv, 3, axis=-1)

        def to_heads(a):
            return a.reshape(b, t, H, D).transpose(0, 2, 1, 3)
        q, k, v = (to_heads(q), to_heads(k), to_heads(v))
        att = jnp.einsum('bhqd,bhkd->bhqk', q, k) * jnp.float32(SCALE)
        allowed = _sliding_window_mask(t, W)
        att = jnp.where(allowed[None, None], att, jnp.float32(-jnp.inf))
        att = jax.nn.softmax(att, axis=-1)
        out = jnp.einsum('bhqk,bhkd->bhqd', att, v)
        out = out.transpose(0, 2, 1, 3).reshape(b, t, e)
        return out @ w_out.T

    def _L0_ffn_ref(input_batch, router_w, w_in, b_in, w_out, b_out):
        import jax, jax.numpy as jnp
        import numpy as np
        D, H, E, K = (128, 128, 8, 2)

        def _moe(x, router_w, w_in, b_in, w_out, b_out):
            B, S, Dm = x.shape
            T = B * S
            x2 = x.reshape(T, Dm)
            logits = x2 @ router_w
            probs = jax.nn.softmax(logits, axis=-1)
            top_p, top_e = jax.lax.top_k(probs, K)
            flat_e = top_e.reshape(-1)
            flat_p = top_p.reshape(-1)
            tok = jnp.repeat(jnp.arange(T), K)
            order = jnp.argsort(flat_e)
            se, sp, st = (flat_e[order], flat_p[order], tok[order])
            xd = x2[st]
            N = xd.shape[0]
            h = jnp.zeros((N, H), x.dtype)
            for e in range(E):
                m = (se == e)[:, None]
                h = h + jnp.where(m, jax.nn.gelu(xd @ w_in[e] + b_in[e]), 0.0)
            y = jnp.zeros((N, Dm), x.dtype)
            for e in range(E):
                m = (se == e)[:, None]
                y = y + jnp.where(m, h @ w_out[e] + b_out[e], 0.0)
            y = y * sp[:, None]
            out = jnp.zeros((T, Dm), x.dtype).at[st].add(y)
            return out.reshape(B, S, Dm)
        return _moe(input_batch, router_w, w_in, b_in, w_out, b_out)
    x = L0_attn_x
    x = _layernorm(x + _L0_attn_ref(x, L0_attn_w_qkv, L0_attn_w_out), axis=-1)
    x = _layernorm(x + _L0_ffn_ref(x, L0_ffn_router_w, L0_ffn_w_in, L0_ffn_b_in, L0_ffn_w_out, L0_ffn_b_out), axis=-1)
    return x

_drawn_inputs = setup_inputs


def setup_inputs(seed=0):
    import zlib

    import numpy as np

    out = dict(_drawn_inputs(seed))
    spreads = {'L0_ffn_b_in': (0.0, 0.28), 'L0_ffn_b_out': (0.0, 0.1)}
    factors = {'L0_attn_w_qkv': 4.406, 'L0_attn_w_out': 3.755}
    for name, (base, spread) in spreads.items():
        noise = np.random.default_rng([zlib.crc32(name.encode()), seed]).standard_normal(out[name].shape)
        drawn = base * np.exp(spread * noise) if base else spread * noise
        out[name] = jnp.asarray(drawn.astype(out[name].dtype))
    for name, factor in factors.items():
        out[name] = (out[name] * factor).astype(out[name].dtype)
    return out
```

```python
import concourse.bass as bass
from concourse import mybir
from contextlib import ExitStack

F32 = mybir.dt.float32
F32R = mybir.dt.float32r
BF16 = mybir.dt.bfloat16
ALU = mybir.AluOpType
ACT = mybir.ActivationFunctionType
X_AXIS = mybir.AxisListType.X

P = 128
B = 8
T = 256
E = 128
H = 16
D = E // H
W = 128
NX = 8
PARTS = 3
BLK = PARTS * D
ROWS = PARTS * BLK
KROWS = ROWS + PARTS
QUADS = H // 4
HALF = H // 2
TILES = B * T // P
CH = 512
CT = CH // P
NCH = B * T // CH
VW = 32
SCALE = 1.0 / float(D) ** 0.5
EPS = 1e-5
MASKED = -(2.0 ** 100)
HEAD = 1


class Batch:

    def __init__(self, pair, parity):
        self.pair, self.parity = pair, parity

    def plus(self, k):
        t = self.parity + k
        return Batch(self.pair + t // 2, t % 2)

    def times(self, per, more=0):
        return self.pair * (2 * per) + (per * self.parity + more)


def wait_apart(engine, semaphore, value, passed):
    engine.wait_ge(semaphore, value)
    engine.sem_inc(passed, 1)


def attention_moe(nc, x_t, x, wqkv_t, wout_t, router_w, w_in, b_in_t, w_out, b_out, out):
    q_scratch = nc.dram_tensor("q_scratch", [2 * PARTS * E, T], BF16, kind="Internal").ap()
    k_scratch = nc.dram_tensor("k_scratch", [2 * (2 * PARTS - 1) * E, T], BF16, kind="Internal").ap()

    with ExitStack() as ctx:
        def sb(name, shape, dt=F32):
            return ctx.enter_context(nc.sbuf_tensor(name, shape, dt))

        def sem(name):
            return ctx.enter_context(nc.semaphore(name))

        bank = [ctx.enter_context(nc.psum_tensor(f"bank{i}", [P, 512], F32)) for i in range(8)]
        score_bank, st_bank, o_bank = bank[0:3], bank[3:5], bank[5]
        misc = bank[6:8]

        ident = sb("ident", [P, P])
        ident_bf = sb("ident_bf", [P, P], BF16)
        mask_first = sb("mask_first", [P, P], BF16)
        mask_second = sb("mask_second", [P, 2, 64], BF16)
        half_power = sb("half_power", [P, CT])
        wqkv_sb = sb("wqkv_sb", [P, 3 * E])
        wout_sb = sb("wout_sb", [P, E])
        router_sb = sb("router_sb", [P, NX])
        b_in_sb = sb("b_in_sb", [P, NX])
        b_out_sb = sb("b_out_sb", [NX, E])
        w_in_sb = sb("w_in_sb", [P, NX, P])
        w_in_hi = sb("w_in_hi", [P, NX, P], F32R)
        w_in_lo = sb("w_in_lo", [P, NX, P], F32R)
        w_out_sb = sb("w_out_sb", [P, NX, E])
        x_t_sb = sb("x_t_sb", [P, B * T])
        xt_sb = [sb(f"x_cols{i}", [P, T]) for i in range(2)]
        x_sb = [sb(f"x_rows{i}", [P, 2, E]) for i in range(2)]
        parts = [sb(f"parts{i}", [P, PARTS, 2, T], BF16) for i in range(2)]
        rest = sb("rest", [P, 2, T])
        qs = [[sb(f"qs{i}{h}", [P, HALF, T], BF16) for h in range(2)] for i in range(2)]
        ks = [[sb(f"ks{i}{h}", [P, HALF, T], BF16) for h in range(2)] for i in range(2)]
        v_sb = [sb(f"v{i}", [P, 2, H, VW]) for i in range(2)]
        neg_max = sb("neg_max", [P, 2, H])
        max_rest = sb("max_rest", [P, 2, HALF])
        max_parts = sb("max_parts", [P, 2, PARTS, HALF], BF16)
        max_t = [sb(f"max_t{h}", [PARTS * HALF, T], BF16) for h in range(2)]
        probs = [sb(f"probs{g}", [P, 3, 4, P]) for g in range(QUADS)]
        o_t = sb("o_t", [P, 2, T])
        inv_sum = sb("inv_sum", [P, 2, H])
        attn = sb("attn", [P, 2, E])
        attn_t = sb("attn_t", [P, T])
        resid = sb("resid", [P, 2, E])
        stats = sb("stats", [P, 2, 6])
        moments = sb("moments", [P, 2, 2])
        var_eps = sb("var_eps", [P, 2])
        rstd = sb("rstd", [P, 2])
        x1 = sb("x1_rows", [P, TILES, E])
        x1_pair = sb("x1_pair", [P, 2, E])
        x1_t = sb("x1_t", [P, T])
        x1_hi = sb("x1_hi", [P, B * T], F32R)
        x1_lo = sb("x1_lo", [P, B * T], F32R)
        logits = sb("logits", [P, TILES, NX])
        route = [sb(f"route{i}", [P, TILES, NX]) for i in range(6)]
        row_stat = [sb(f"row_stat{i}", [P, TILES]) for i in range(6)]
        rank_w = sb("rank_w", [P, TILES, NX])
        gate = sb("gate", [P, TILES, NX])
        gate_c = sb("gate_c", [P, CT, NX])
        gate_t = sb("gate_t", [NX, CH])
        hid = [sb(f"hid{i}", [P, CH]) for i in range(2)]
        acc = sb("acc", [P, CT, E])
        stats2 = sb("stats2", [P, CT, 6])
        moments2 = sb("moments2", [P, CT, 2])
        var2 = sb("var2", [P, CT])
        rstd2 = sb("rstd2", [P, CT])
        y_sb = sb("y_sb", [P, CT, E])

        qkv_w_loaded, out_w_loaded, moe_w_loaded = sem("qkv_w_loaded"), sem("out_w_loaded"), sem("moe_w_loaded")
        x_t_loaded = [sem(f"x_t_loaded{i}") for i in range(2)]
        xt_loaded = [sem(f"xt_loaded{i}") for i in range(2)]
        x_loaded = [sem(f"x_loaded{i}") for i in range(2)]
        consts_ready = sem("consts_ready")
        sp_passed, pool_passed, dve_passed = sem("sp_passed"), sem("pool_passed"), sem("dve_passed")
        base_ready, ones_ready = sem("base_ready"), sem("ones_ready")
        v_zeroed, v_ones = sem("v_zeroed"), sem("v_ones")
        maxima, x1_kept = sem("maxima"), sem("x1_kept")
        qk_projected, v_projected = sem("qk_projected"), sem("v_projected")
        part_top, part_rest, part_mid, part_low = sem("part_top"), sem("part_rest"), sem("part_mid"), sem("part_low")
        scratch_written = [sem(f"scratch_written{i}") for i in range(2)]
        stacked = [[sem(f"stacked{i}{h}") for h in range(2)] for i in range(2)]
        v_padded = sem("v_padded")
        scores_ready = sem("scores_ready")
        max_top, max_rested, max_mid, max_split = sem("max_top"), sem("max_rested"), sem("max_mid"), sem("max_split")
        max_turned, max_copied = sem("max_turned"), sem("max_copied")
        max_stacked = [[sem(f"max_stacked{i}{h}") for h in range(2)] for i in range(2)]
        st_ready, exp_done, masked, pv_done = sem("st_ready"), sem("exp_done"), sem("masked"), sem("pv_done")
        o_copied, o_turned, sums_inverted, normed = sem("o_copied"), sem("o_turned"), sem("sums_inverted"), sem("normed")
        attn_turned, attn_copied, projected = sem("attn_turned"), sem("attn_copied"), sem("projected")
        resid_done, stats_done, moments_done = sem("resid_done"), sem("stats_done"), sem("moments_done")
        eps_added, rstd_done, x1_done = sem("eps_added"), sem("rstd_done"), sem("x1_done")
        x1_turned, x1_copied, x1_hi_done, x1_lo_done = sem("x1_turned"), sem("x1_copied"), sem("x1_hi_done"), sem("x1_lo_done")
        logits_ready, logits_copied = sem("logits_ready"), sem("logits_copied")
        w_hi_done, w_lo_done = sem("w_hi_done"), sem("w_lo_done")
        routing, route_shifted, route_exp, gate_done = sem("routing"), sem("route_shifted"), sem("route_exp"), sem("gate_done")
        rank_ready = sem("rank_ready")
        gate_staged, gate_turned, gate_copied, bias_ready = sem("gate_staged"), sem("gate_turned"), sem("gate_copied"), sem("bias_ready")
        hid_ready, gelu_done, y_ready, y_added = sem("hid_ready"), sem("gelu_done"), sem("y_ready"), sem("y_added")
        acc_started, stats2_done, moments2_done = sem("acc_started"), sem("stats2_done"), sem("moments2_done")
        eps2_added, rstd2_done, y_normed, stored = sem("eps2_added"), sem("rstd2_done"), sem("y_normed"), sem("stored")

        block = ctx.enter_context(nc.Block())

        FULL = dict(proj=True, score=True, prob=True, tail=True, turn=True, pv_last=True)
        STEPS_BEFORE = [
            (0, dict(FULL, prob=False, tail=False, turn=False, pv_last=False)),
            (1, dict(FULL, tail=False, turn=False, pv_last=False)),
            (2, dict(FULL, turn=False)),
        ]
        LOOP_STEPS = (3, 7)
        STEPS_AFTER = [
            (7, dict(FULL, proj=False)),
            (8, dict(FULL, proj=False, score=False)),
            (9, dict(FULL, proj=False, score=False, prob=False)),
            (10, dict(FULL, proj=False, score=False, prob=False, tail=False, pv_last=False)),
        ]

        def all_steps(engine, step):
            for s, on in STEPS_BEFORE:
                step(Batch(s // 2, s % 2), on, s)
            with engine.Fori(LOOP_STEPS[0] // 2, LOOP_STEPS[1] // 2) as pair:
                step(Batch(pair, 1), FULL, None)
                step(Batch(pair, 1).plus(1), FULL, None)
            for s, on in STEPS_AFTER:
                step(Batch(s // 2, s % 2), on, s)

        @block.sync
        def _(sp):
            def load_xt(b):
                sp.dma_start(xt_sb[b.parity][:, :], x_t[:, bass.ds(b.times(T), T)]).then_inc(xt_loaded[b.parity], 16)

            def load_x(b):
                sp.dma_start(x_sb[b.parity][:, :, :],
                             x[bass.ds(b.times(T), T), :].rearrange("(n p) e -> p n e", p=P)) \
                    .then_inc(x_loaded[b.parity], 16)

            def write_parts(b):
                par = b.parity
                q0, k0 = par * PARTS * E, par * (2 * PARTS - 1) * E
                sp.wait_ge(part_low, b.times(1, 1))
                sp.dma_start(q_scratch[q0:q0 + PARTS * E, :].rearrange("(a r) t -> r a t", a=PARTS),
                             parts[par][:, :, 0, :]).then_inc(scratch_written[par], 16)
                sp.dma_start(k_scratch[k0:k0 + PARTS * E, :].rearrange("(a r) t -> r a t", a=PARTS),
                             parts[par][:, :, 1, :]).then_inc(scratch_written[par], 16)
                sp.dma_start(k_scratch[k0 + PARTS * E:k0 + (2 * PARTS - 1) * E, :]
                             .rearrange("(a r) t -> r a t", a=PARTS - 1),
                             parts[par][:, 0:PARTS - 1, 1, :]).then_inc(scratch_written[par], 16)
                wait_apart(sp, scratch_written[par], b.pair * 48 + 48, sp_passed)

            def stack(b, h, in_use):
                par = b.parity
                if in_use:
                    sp.wait_ge(st_ready, b.plus(-2).times(H, HALF * (h + 1)))
                for scratch, operand, copies, step_r in ((q_scratch, qs, PARTS, 0), (k_scratch, ks, 2 * PARTS - 1, D * H * T)):
                    at = par * copies * E * T + h * HALF * T
                    sp.dma_start(operand[par][h][0:ROWS, :, :],
                                 bass.AP(scratch.tensor, scratch.offset + at, [[step_r, PARTS], [H * T, BLK], [1, HALF * T]])) \
                        .then_inc(stacked[par][h], 16)

            def stack_max(b, h):
                sp.wait_ge(max_copied, b.times(2, h + 1))
                sp.dma_start(qs[b.parity][h][ROWS:KROWS, :, :], max_t[h][:, :]).then_inc(max_stacked[b.parity][h], 16)

            sp.sem_inc(stored, HEAD)
            b0, b1 = Batch(0, 0), Batch(0, 1)
            sp.dma_start(wqkv_sb[:, :], wqkv_t).then_inc(qkv_w_loaded, 16)
            sp.dma_start(x_t_sb[:, 0:2 * T], x_t[:, 0:2 * T]).then_inc(x_t_loaded[0], 16)
            load_xt(b0)
            sp.dma_start(wout_sb[:, :], wout_t).then_inc(out_w_loaded, 16)
            load_x(b0)
            load_x(b1)
            sp.dma_start(router_sb[:, :], router_w).then_inc(moe_w_loaded, 16)
            sp.dma_start(b_in_sb[:, :], b_in_t).then_inc(moe_w_loaded, 16)
            sp.dma_start(b_out_sb[:, :], b_out).then_inc(moe_w_loaded, 16)
            sp.dma_start(x_t_sb[:, 2 * T:B * T], x_t[:, 2 * T:B * T]).then_inc(x_t_loaded[1], 16)
            sp.wait_ge(ones_ready, 1)
            write_parts(b0)
            stack(b0, 0, False)
            stack(b0, 1, False)
            sp.dma_start(w_in_sb[:, :, :], w_in.rearrange("e d h -> d e h")).then_inc(moe_w_loaded, 16)
            sp.dma_start(w_out_sb[:, :, :], w_out.rearrange("e h d -> h e d")).then_inc(moe_w_loaded, 16)

            def step(s, on, n):
                if on["prob"]:
                    stack_max(s.plus(-1), 1)
                if on["proj"]:
                    if n is None or n >= 1:
                        wait_apart(sp, v_projected, s.plus(-1).times(1, 1), sp_passed)
                    load_xt(s.plus(1))
                if on["proj"]:
                    write_parts(s.plus(1))
                    stack(s.plus(1), 0, n is None or n >= 1)
                if on["score"]:
                    stack_max(s, 0)
                if on["proj"]:
                    stack(s.plus(1), 1, n is None or n >= 1)
                if n is None or 2 <= n < B:
                    wait_apart(sp, resid_done, s.plus(-2).times(1, 1), sp_passed)
                    load_x(s)

            all_steps(sp, step)
            with sp.Fori(0, NCH) as c:
                wait_apart(sp, y_normed, c * CT + CT, sp_passed)
                sp.dma_start(out[bass.ds(c * CH, CH), :].rearrange("(n p) e -> p n e", p=P), y_sb[:, :, :]) \
                    .then_inc(stored, 16)
            sp.wait_ge(stored, NCH * 16 + HEAD)

        @block.gpsimd
        def _(pool):
            pool.sem_inc(x1_kept, HEAD)
            pool.memset(ident[:, :], 0.0).then_inc(base_ready, 1)
            pool.memset(ident_bf[:, :], 0.0).then_inc(base_ready, 1)
            pool.memset(mask_first[:, :], 0.0).then_inc(base_ready, 1)
            pool.memset(mask_second[:, :, :], 0.0).then_inc(base_ready, 1)
            pool.memset(half_power[:, :], -0.5).then_inc(base_ready, 1)
            pool.wait_ge(base_ready, 5)
            for m in (ident, ident_bf):
                pool.affine_select(out=m[:, :], in_=m[:, :], compare_op=ALU.not_equal, fill=1.0, base=0,
                                   pattern=[[-1, P]], channel_multiplier=1).then_inc(consts_ready, 1)
            pool.affine_select(out=mask_first[:, :], in_=mask_first[:, :], compare_op=ALU.is_ge, fill=MASKED, base=0,
                               pattern=[[-1, P]], channel_multiplier=1).then_inc(consts_ready, 1)
            for lo in (0, 64):
                pool.wait_ge(consts_ready, 3 + lo // 32)
                part = mask_second[lo:lo + 64, 0, :]
                pool.affine_select(out=part, in_=part, compare_op=ALU.is_gt, fill=MASKED, base=0,
                                   pattern=[[1, 64]], channel_multiplier=-1).then_inc(consts_ready, 1)
                part = mask_second[lo:lo + 64, 1, :]
                pool.affine_select(out=part, in_=part, compare_op=ALU.is_ge, fill=MASKED, base=0,
                                   pattern=[[-1, 64]], channel_multiplier=1).then_inc(consts_ready, 1)
            pool.wait_ge(consts_ready, 7)
            for par in range(2):
                pool.memset(v_sb[par][:, :, :, :], 0.0).then_inc(v_zeroed, 1)
            pool.wait_ge(v_zeroed, 2)
            for par in range(2):
                for kt in range(2):
                    for s in range(2):
                        ones = v_sb[par][:, kt, :, :].rearrange("p (t s j) c -> p t s j c", t=2, s=2)[:, :, s, :, (D + 1) * s + D]
                        pool.memset(ones, 1.0).then_inc(v_ones, 1)
            for e in range(NX):
                pool.memset(rank_w[:, :, e:e + 1], float(NX - e)).then_inc(rank_ready, 1)

            def step(s, on, n):
                for g in range(QUADS):
                    if on["prob"]:
                        b = s.plus(-1)
                        wait_apart(pool, exp_done, b.times(H, 4 * g + 4), pool_passed)
                        own, other = probs[g][:, 0:3:2, :, :], probs[g][:, 1, :, :]
                        pool.affine_select(out=own, in_=own, compare_op=ALU.is_ge,
                                           fill=0.0, base=0, pattern=[[0, 2], [0, 4], [1, P]],
                                           channel_multiplier=-1).then_inc(masked, 1)
                        pool.affine_select(out=other, in_=other, compare_op=ALU.is_gt,
                                           fill=0.0, base=0, pattern=[[0, 4], [-1, P]],
                                           channel_multiplier=1).then_inc(masked, 1)
                    if g == 0 and on["turn"]:
                        b = s.plus(-3)
                        pool.wait_ge(x1_done, b.times(2, 2))
                        pool.tensor_copy(x1[:, bass.ds(b.times(2), 2), :], x1_pair[:, :, :]).then_inc(x1_kept, 1)
                if on["tail"]:
                    b = s.plus(-2)
                    wait_apart(pool, moments_done, b.times(2, 2), pool_passed)
                    pool.tensor_scalar(var_eps[:, :], moments[:, :, 1], EPS, None, ALU.add).then_inc(eps_added, 1)
                    pool.wait_ge(eps_added, b.times(1, 1))
                    pool.tensor_tensor(rstd[:, :], var_eps[:, :], half_power[:, 0:2], ALU.pow).then_inc(rstd_done, 1)

            all_steps(pool, step)
            with pool.Fori(0, NCH) as c:
                wait_apart(pool, moments2_done, c * CT + CT, pool_passed)
                pool.tensor_scalar(var2[:, :], moments2[:, :, 1], EPS, None, ALU.add).then_inc(eps2_added, 1)
                pool.wait_ge(eps2_added, c + 1)
                pool.tensor_tensor(rstd2[:, :], var2[:, :], half_power[:, :], ALU.pow).then_inc(rstd2_done, 1)

        @block.scalar
        def _(act):
            def step(s, on, n):
                for g in range(QUADS):
                    if on["prob"]:
                        b = s.plus(-1)
                        for i in range(4):
                            k = 4 * g + i
                            if i == 0 and (n is None or n >= 2):
                                act.wait_ge(pv_done, b.plus(-1).times(QUADS, g + 1))
                            act.wait_ge(st_ready, b.times(H, k + 1))
                            nc.scalar.activation(probs[g][:, :, i, :], st_bank[k % 2][:, 0:3 * P].rearrange("p (k c) -> p k c", k=3), ACT.Exp, scale=SCALE) \
                                .then_inc(exp_done, 1)
                    if g == 0 and on["prob"]:
                        b = s.plus(-1)
                        act.wait_ge(max_turned, b.times(2, 2))
                        if n is None or n >= 2:
                            act.wait_ge(max_stacked[b.plus(-1).parity][1], b.plus(-1).pair * 16 + 16)
                        nc.scalar.activation(max_t[1][:, :], misc[0][0:PARTS * HALF, :].bitcast(BF16)[:, 0:T], ACT.Copy).then_inc(max_copied, 1)
                    if g == 0 and on["proj"]:
                        b = s.plus(1)
                        take_top(b, n is None or n >= 1)
                    if g == 0 and on["pv_last"]:
                        b = s.plus(-2)
                        act.wait_ge(pv_done, b.times(QUADS, QUADS))
                        if n is None or n >= 3:
                            act.wait_ge(o_turned, b.plus(-1).times(1, 1))
                        nc.scalar.activation(o_t[:, :, :], o_bank[:, :].rearrange("p (t q) -> p t q", t=2), ACT.Copy).then_inc(o_copied, 1)
                    if g == 1 and on["score"]:
                        pad_v(s, n is None or n >= 2)
                    if g == 2 and on["score"]:
                        act.wait_ge(max_turned, s.times(2, 1))
                        if n is None or n >= 1:
                            act.wait_ge(max_stacked[s.plus(-1).parity][0], s.plus(-1).pair * 16 + 16)
                        nc.scalar.activation(max_t[0][:, :], misc[0][0:PARTS * HALF, :].bitcast(BF16)[:, 0:T], ACT.Copy).then_inc(max_copied, 1)
                    if g == 2 and on["tail"]:
                        act.wait_ge(attn_turned, s.plus(-2).times(1, 1))
                        if n is None or n >= 3:
                            act.wait_ge(projected, s.plus(-3).times(1, 1))
                        nc.scalar.activation(attn_t[:, :], misc[0][:, 0:T], ACT.Copy).then_inc(attn_copied, 1)
                    if g == 2 and on["turn"]:
                        b = s.plus(-3)
                        act.wait_ge(x1_turned, b.times(1, HEAD + 1))
                        if n is None or n >= 4:
                            act.wait_ge(x1_lo_done, b.times(1, HEAD))
                            act.wait_ge(logits_ready, b.times(1, HEAD))
                        nc.scalar.activation(x1_t[:, :], misc[1][:, 0:T], ACT.Copy).then_inc(x1_copied, 1)
                    if g == 3 and on["turn"]:
                        b = s.plus(-3)
                        act.wait_ge(logits_ready, b.times(1, HEAD + 1))
                        nc.scalar.activation(logits[:, bass.ds(b.times(2), 2), :],
                                             misc[1][:, 0:2 * NX].rearrange("p (n e) -> p n e", n=2), ACT.Copy).then_inc(logits_copied, 1)

            def take_top(b, in_use):
                act.wait_ge(qk_projected, b.times(1, 1))
                if in_use:
                    act.wait_ge(scratch_written[b.parity], b.plus(-2).pair * 48 + 48)
                nc.scalar.activation(parts[b.parity][:, 0, :, :], misc[0][:, :].rearrange("p (a t) -> p a t", a=2), ACT.Copy).then_inc(part_top, 1)

            def pad_v(b, in_use):
                act.wait_ge(v_projected, b.times(1, 1))
                if in_use:
                    act.wait_ge(pv_done, b.plus(-2).times(QUADS, QUADS))
                else:
                    act.wait_ge(v_ones, 8)
                for kt in range(2):
                    for s in range(2):
                        dst = v_sb[b.parity][:, kt, :, (D + 1) * s:(D + 1) * s + D].rearrange("p (t s j) c -> p t s j c", t=2, s=2)[:, :, s, :, :]
                        src = misc[1][:, kt * E:(kt + 1) * E].rearrange("p (t s j c) -> p t s j c", t=2, s=2, j=4)[:, :, s, :, :]
                        nc.scalar.activation(dst, src, ACT.Copy).then_inc(v_padded, 1)

            for count in (gelu_done, logits_copied):
                act.sem_inc(count, HEAD)
            take_top(Batch(0, 0), False)
            all_steps(act, step)

            act.wait_ge(route_shifted, 1)
            nc.scalar.activation(route[1][:, :, :], route[0][:, :, :], ACT.Exp).then_inc(route_exp, 1)
            with act.Fori(0, NCH) as c:
                for e in range(NX):
                    act.wait_ge(hid_ready, c * NX + (e + 1))
                    if e >= 2:
                        act.wait_ge(y_ready, c * NX + (HEAD + e - 1))
                    else:
                        act.wait_ge(y_ready, c * NX + HEAD)
                    nc.scalar.activation(hid[e % 2][:, :], bank[e % 2][:, :], ACT.Gelu_apprx_tanh,
                                         bias=b_in_sb[:, e:e + 1]).then_inc(gelu_done, 1)
                    if e == 0:
                        act.wait_ge(gate_turned, c + 1)
                        nc.scalar.activation(gate_t[:, :], bank[4][0:NX, :], ACT.Copy).then_inc(gate_copied, 1)

        @block.vector
        def _(dve):
            def split_rest(b):
                p = parts[b.parity]
                dve.wait_ge(part_top, b.times(1, 1))
                nc.vector.tensor_tensor(rest[:, :, :], misc[0][:, :].rearrange("p (a t) -> p a t", a=2), p[:, 0, :, :],
                                        ALU.subtract).then_inc(part_rest, 1)
                dve.wait_ge(part_rest, b.times(1, 1))
                nc.vector.tensor_copy(p[:, 1, :, :], rest[:, :, :]).then_inc(part_mid, 1)
                dve.wait_ge(part_mid, b.times(1, 1))
                nc.vector.tensor_tensor(p[:, 2, :, :], rest[:, :, :], p[:, 1, :, :], ALU.subtract).then_inc(part_low, 1)

            def split_max(b, h, in_use):
                full = neg_max[:, :, h * HALF:(h + 1) * HALF]
                k = b.times(2, h + 1)
                dve.wait_ge(maxima, b.times(3 * QUADS, 3 * (QUADS // 2) * (h + 1)))
                if in_use:
                    dve.wait_ge(max_turned, b.times(2, h))
                nc.vector.tensor_copy(max_parts[:, :, 0, :], full).then_inc(max_top, 1)
                dve.wait_ge(max_top, k)
                nc.vector.tensor_tensor(max_rest[:, :, :], full, max_parts[:, :, 0, :], ALU.subtract).then_inc(max_rested, 1)
                dve.wait_ge(max_rested, k)
                nc.vector.tensor_copy(max_parts[:, :, 1, :], max_rest[:, :, :]).then_inc(max_mid, 1)
                dve.wait_ge(max_mid, k)
                nc.vector.tensor_tensor(max_parts[:, :, 2, :], max_rest[:, :, :], max_parts[:, :, 1, :], ALU.subtract).then_inc(max_split, 1)

            def normalise(b):
                turned = misc[1][:, :].rearrange("p (n t j c) -> p n t j c", n=2, t=2, j=4)
                dve.wait_ge(o_turned, b.times(1, 1))
                for n in range(2):
                    nc.vector.reciprocal(inv_sum[:, n, :].rearrange("p (t s j) -> p t j s", t=2, s=2),
                                         turned[:, n, :, :, D:2 * (D + 1):D + 1]).then_inc(sums_inverted, 1)
                dve.wait_ge(sums_inverted, b.times(2, 2))
                for n in range(2):
                    for t in range(2):
                        src = turned[:, n, t, :, 0:2 * (D + 1)].rearrange("p j (s c) -> p s j c", s=2)[:, :, :, 0:D]
                        inv = inv_sum[:, n, t * HALF:(t + 1) * HALF].rearrange("p (s j) -> p s j", s=2).unsqueeze(3).to_broadcast([P, 2, 4, D])
                        dst = attn[:, n, t * 64:(t + 1) * 64].rearrange("p (s j c) -> p s j c", s=2, j=4)
                        nc.vector.tensor_tensor(dst, src, inv, ALU.mult).then_inc(normed, 1)

            def first_residual(b):
                dve.wait_ge(projected, b.times(1, 1))
                dve.wait_ge(x_loaded[b.parity], b.pair * 16 + 16)
                nc.vector.tensor_tensor(resid[:, :, :], misc[1][:, 0:T].rearrange("p (n e) -> p n e", n=2),
                                        x_sb[b.parity][:, :, :], ALU.add).then_inc(resid_done, 1)
                dve.wait_ge(resid_done, b.times(1, 1))
                for n in range(2):
                    nc.vector.bn_stats(stats[:, n, :], resid[:, n, :]).then_inc(stats_done, 1)
                wait_apart(dve, stats_done, b.times(2, 2), dve_passed)
                for n in range(2):
                    nc.vector.bn_aggr(moments[:, n, :], stats[:, n, :]).then_inc(moments_done, 1)

            def first_norm(b, in_use):
                dve.wait_ge(rstd_done, b.times(1, 1))
                if in_use:
                    dve.wait_ge(x1_kept, b.times(1, HEAD))
                    dve.wait_ge(x1_turned, b.times(1, HEAD))
                for n in range(2):
                    nc.vector.tensor_scalar(x1_pair[:, n, :], resid[:, n, :], moments[:, n, 0:1], rstd[:, n:n + 1],
                                            ALU.subtract, ALU.mult).then_inc(x1_done, 1)

            def split_x1(b):
                cols = bass.ds(b.times(T), T)
                dve.wait_ge(x1_copied, b.times(1, 1))
                nc.vector.tensor_copy(x1_hi[:, cols], x1_t[:, :]).then_inc(x1_hi_done, 1)
                dve.wait_ge(x1_hi_done, b.times(1, 1))
                nc.vector.tensor_tensor(x1_lo[:, cols], x1_t[:, :], x1_hi[:, cols].bitcast(F32), ALU.subtract).then_inc(x1_lo_done, 1)

            def step(s, on, n):
                for g in range(QUADS):
                    if on["score"]:
                        k = s.times(3 * QUADS, 3 * g)
                        if g == 0 and (n is None or n >= 1):
                            dve.wait_ge(max_split, s.plus(-1).times(2, 2))
                        dve.wait_ge(scores_ready, k + 1)
                        nc.vector.tensor_reduce(neg_max[:, 0, 4 * g:4 * g + 4], score_bank[0][:, :].rearrange("p (h c) -> p h c", h=4),
                                                X_AXIS, ALU.max, negate=True).then_inc(maxima, 1)
                        for u in range(2):
                            dve.wait_ge(scores_ready, k + (2 + u))
                            nc.vector.tensor_reduce(neg_max[:, 1, 4 * g + 2 * u:4 * g + 2 * u + 2],
                                                    score_bank[1 + u][:, 0:384].rearrange("p (h c) -> p h c", h=2),
                                                    X_AXIS, ALU.max, negate=True).then_inc(maxima, 1)
                        if g == 1:
                            split_max(s, 0, n is None or n >= 1)
                        if g == 3:
                            split_max(s, 1, True)
                    if g == 0 and on["turn"]:
                        first_norm(s.plus(-3), n is None or n >= 4)
                    if g == 0 and on["proj"]:
                        split_rest(s.plus(1))
                    if g == 1 and on["tail"]:
                        normalise(s.plus(-2))
                    if g == 2 and on["turn"]:
                        split_x1(s.plus(-3))
                    if g == 3 and on["tail"]:
                        first_residual(s.plus(-2))

            for count in (y_added, x1_lo_done):
                dve.sem_inc(count, HEAD)
            for par in range(2):
                for h in range(2):
                    last = nc.vector.memset(ks[par][h][64:P, :, :], 1.0)
            last.then_inc(ones_ready, 1)
            split_rest(Batch(0, 0))
            dve.wait_ge(moe_w_loaded, 16 * 5)
            nc.vector.tensor_copy(w_in_hi[:, :, :], w_in_sb[:, :, :]).then_inc(w_hi_done, 1)
            dve.wait_ge(w_hi_done, 1)
            nc.vector.tensor_tensor(w_in_lo[:, :, :], w_in_sb[:, :, :], w_in_hi[:, :, :].bitcast(F32), ALU.subtract).then_inc(w_lo_done, 1)
            all_steps(dve, step)

            links = 0

            def link(ins):
                nonlocal links
                links += 1
                ins.then_inc(routing, 1)
                dve.wait_ge(routing, links)

            def wide(ap):
                return ap[:, :].unsqueeze(2).to_broadcast([P, TILES, NX])

            dve.wait_ge(logits_copied, HEAD + B)
            link(nc.vector.tensor_reduce(row_stat[0][:, :], logits[:, :, :], X_AXIS, ALU.max))
            nc.vector.tensor_tensor(route[0][:, :, :], logits[:, :, :], wide(row_stat[0]), ALU.subtract).then_inc(route_shifted, 1)
            dve.wait_ge(route_exp, 1)
            link(nc.vector.tensor_reduce(row_stat[1][:, :], route[1][:, :, :], X_AXIS, ALU.add))
            link(nc.vector.reciprocal(row_stat[2][:, :], row_stat[1][:, :]))
            link(nc.vector.tensor_tensor(route[0][:, :, :], route[1][:, :, :], wide(row_stat[2]), ALU.mult))
            dve.wait_ge(rank_ready, NX)

            def first_largest(p, one_hot):
                link(nc.vector.tensor_reduce(row_stat[3][:, :], p, X_AXIS, ALU.max))
                link(nc.vector.tensor_tensor(route[4][:, :, :], p, wide(row_stat[3]), ALU.is_equal))
                link(nc.vector.tensor_tensor(route[4][:, :, :], route[4][:, :, :], rank_w[:, :, :], ALU.mult))
                link(nc.vector.tensor_reduce(row_stat[4][:, :], route[4][:, :, :], X_AXIS, ALU.max))
                link(nc.vector.tensor_tensor(one_hot, route[4][:, :, :], wide(row_stat[4]), ALU.is_equal))

            first_largest(route[0][:, :, :], route[2][:, :, :])
            link(nc.vector.scalar_tensor_tensor(route[3][:, :, :], route[2][:, :, :], -2.0, route[0][:, :, :], ALU.mult, ALU.add))
            first_largest(route[3][:, :, :], route[5][:, :, :])
            link(nc.vector.tensor_tensor(route[5][:, :, :], route[5][:, :, :], route[2][:, :, :], ALU.add))
            nc.vector.tensor_tensor(gate[:, :, :], route[5][:, :, :], route[0][:, :, :], ALU.mult).then_inc(gate_done, 1)
            dve.wait_ge(gate_done, 1)
            dve.wait_ge(x1_kept, HEAD + B)

            with dve.Fori(0, NCH) as c:
                nc.vector.tensor_copy(gate_c[:, :, :], gate[:, bass.ds(c * CT, CT), :]).then_inc(gate_staged, 1)
                dve.wait_ge(bias_ready, c + 1)
                nc.vector.tensor_tensor(acc[:, :, :], bank[5][:, :].rearrange("p (n e) -> p n e", n=CT),
                                        x1[:, bass.ds(c * CT, CT), :], ALU.add).then_inc(acc_started, 1)
                dve.wait_ge(acc_started, c + 1)
                for e in range(NX):
                    dve.wait_ge(y_ready, c * NX + (HEAD + e + 1))
                    if e:
                        dve.wait_ge(y_added, c * (NX * CT) + (HEAD + e * CT))
                    for n in range(CT):
                        nc.vector.scalar_tensor_tensor(acc[:, n, :], bank[2 + e % 2][:, n * E:(n + 1) * E], gate_c[:, n, e:e + 1],
                                                       acc[:, n, :], ALU.mult, ALU.add).then_inc(y_added, 1)
                dve.wait_ge(y_added, c * (NX * CT) + (HEAD + NX * CT))
                for n in range(CT):
                    nc.vector.bn_stats(stats2[:, n, :], acc[:, n, :]).then_inc(stats2_done, 1)
                wait_apart(dve, stats2_done, c * CT + CT, dve_passed)
                for n in range(CT):
                    nc.vector.bn_aggr(moments2[:, n, :], stats2[:, n, :]).then_inc(moments2_done, 1)
                dve.wait_ge(rstd2_done, c + 1)
                dve.wait_ge(stored, c * 16 + HEAD)
                for n in range(CT):
                    nc.vector.tensor_scalar(y_sb[:, n, :], acc[:, n, :], moments2[:, n, 0:1], rstd2[:, n:n + 1],
                                            ALU.subtract, ALU.mult).then_inc(y_normed, 1)

        @block.tensor
        def _(pe):
            mm = nc.tensor.matmul

            def project_qk(b):
                for a in range(2):
                    last = mm(misc[0][:, a * T:(a + 1) * T], wqkv_sb[:, a * E:(a + 1) * E], x_t_sb[:, bass.ds(b.times(T), T)], start=True, stop=True)
                last.then_inc(qk_projected, 1)

            def project_v(b):
                pe.wait_ge(xt_loaded[b.parity], b.pair * 16 + 16)
                for kt in range(2):
                    last = mm(misc[1][:, kt * E:(kt + 1) * E], xt_sb[b.parity][:, kt * P:(kt + 1) * P], wqkv_sb[:, 2 * E:3 * E], start=True, stop=True)
                last.then_inc(v_projected, 1)

            def scores(b, g, in_use):
                q, k = qs[b.parity][g // 2], ks[b.parity][g // 2]
                if g % 2 == 0:
                    pe.wait_ge(stacked[b.parity][g // 2], b.pair * 32 + 32)
                done = b.times(3 * QUADS, 3 * g)
                if in_use:
                    pe.wait_ge(maxima, done - 2)
                mm(score_bank[0][:, :], ident_bf[:, :], mask_first[:, :].unsqueeze(1).to_broadcast([P, 4, P]), start=True, stop=True)
                for i in range(4):
                    h = 4 * (g % 2) + i
                    last = mm(score_bank[0][:, i * P:(i + 1) * P], q[0:ROWS, h, 0:P], k[0:ROWS, h, 0:P], start=False, stop=True, skip_group_check=True)
                last.then_inc(scores_ready, 1)
                for u in range(2):
                    bank_u = score_bank[1 + u]
                    if in_use:
                        pe.wait_ge(maxima, done - (1 - u))
                    edges = bank_u[:, 0:384].rearrange("p (h a c) -> p h a c", h=2, a=3)[:, :, 0:3:2, :]
                    mm(edges, ident_bf[:, :], mask_second[:, :, :].unsqueeze(1).to_broadcast([P, 2, 2, 64]), start=True, stop=True)
                    for i in range(2):
                        h = 4 * (g % 2) + 2 * u + i
                        for half in range(2):
                            lo = 64 * half
                            last = mm(bank_u[lo:lo + 64, i * 192:(i + 1) * 192], q[0:ROWS, h, P + lo:P + lo + 64], k[0:ROWS, h, lo:lo + 192],
                                      start=False, stop=True, skip_group_check=True)
                    last.then_inc(scores_ready, 1)

            def turned_scores(b, g, started):
                q, k = qs[b.parity][g // 2], ks[b.parity][g // 2]
                if g % 2 == 0:
                    pe.wait_ge(max_stacked[b.parity][g // 2], b.pair * 16 + 16)
                for i in range(4):
                    n, h = 4 * g + i, 4 * (g % 2) + i
                    if started or n >= 2:
                        pe.wait_ge(exp_done, b.times(H, n - 1))
                    out_bank = st_bank[n % 2]
                    mm(out_bank[:, 0:T], k[0:KROWS, h, 0:P], q[0:KROWS, h, :], start=True, stop=True)
                    mm(out_bank[:, T:T + P], k[0:KROWS, h, P:T], q[0:KROWS, h, P:T], start=True, stop=True).then_inc(st_ready, 1)

            def weigh_values(b, g):
                t, s = g // 2, g % 2
                pe.wait_ge(masked, b.times(2 * QUADS, 2 * g + 2))
                if g == 0:
                    pe.wait_ge(v_padded, b.times(4, 4))
                for kt in range(2):
                    for j in range(4):
                        h = 4 * g + j
                        v = v_sb[b.parity][:, kt, h, :]
                        rows = slice(VW * j, VW * (j + 1))
                        if kt == 0:
                            last = mm(o_bank[rows, t * T:(t + 1) * T], v, probs[g][:, 0:2, j, :], start=s == 0, stop=s == 1, skip_group_check=True)
                        else:
                            last = mm(o_bank[rows, t * T + P:(t + 1) * T], v, probs[g][:, 2, j, :], start=False, stop=s == 1, skip_group_check=True)
                last.then_inc(pv_done, 1)

            def turn_max(b, h):
                turned = misc[0][0:PARTS * HALF, :].bitcast(BF16)
                pe.wait_ge(max_split, b.times(2, h + 1))
                for n in range(2):
                    last = nc.tensor.transpose(turned[:, n * P:(n + 1) * P], max_parts[:, n, :, :].rearrange("p a h -> p (a h)"), ident_bf[:, :])
                last.then_inc(max_turned, 1)

            def turn_output(b):
                pe.wait_ge(o_copied, b.times(1, 1))
                for n in range(2):
                    for t in range(2):
                        last = nc.tensor.transpose(misc[1][:, (2 * n + t) * P:(2 * n + t + 1) * P], o_t[:, t, n * P:(n + 1) * P], ident[:, :])
                last.then_inc(o_turned, 1)

            def turn_attention(b):
                pe.wait_ge(normed, b.times(4, 4))
                for n in range(2):
                    last = nc.tensor.transpose(misc[0][:, n * P:(n + 1) * P], attn[:, n, :], ident[:, :])
                last.then_inc(attn_turned, 1)

            def project_out(b):
                pe.wait_ge(attn_copied, b.times(1, 1))
                for n in range(2):
                    last = mm(misc[1][:, n * E:(n + 1) * E], attn_t[:, n * P:(n + 1) * P], wout_sb[:, :], start=True, stop=True)
                last.then_inc(projected, 1)

            def turn_x1(b):
                pe.wait_ge(x1_done, b.times(2, 2))
                for n in range(2):
                    last = nc.tensor.transpose(misc[1][:, n * P:(n + 1) * P], x1_pair[:, n, :], ident[:, :])
                last.then_inc(x1_turned, 1)

            def route_logits(b):
                pe.wait_ge(x1_copied, b.times(1, 1))
                for n in range(2):
                    last = mm(misc[1][:, n * NX:(n + 1) * NX], x1_t[:, n * P:(n + 1) * P], router_sb[:, :], start=True, stop=True)
                last.then_inc(logits_ready, 1)

            for count in (y_ready, x1_turned, logits_ready):
                pe.sem_inc(count, HEAD)
            pe.wait_ge(qkv_w_loaded, 16)
            pe.wait_ge(x_t_loaded[0], 16)
            project_qk(Batch(0, 0))
            pe.wait_ge(consts_ready, 7)
            pe.wait_ge(ones_ready, 1)
            pe.wait_ge(out_w_loaded, 16)

            def step(s, on, n):
                loop = n is None
                for g in range(QUADS):
                    if on["score"]:
                        scores(s, g, loop or n > 0 or g > 0)
                    if on["prob"]:
                        turned_scores(s.plus(-1), g, loop or n > 1)
                    if g == 0 and on["pv_last"]:
                        weigh_values(s.plus(-2), QUADS - 1)
                    if g > 0 and on["prob"]:
                        if g == 1 and (loop or n > 1):
                            pe.wait_ge(o_copied, s.plus(-2).times(1, 1))
                        weigh_values(s.plus(-1), g - 1)
                    if g == 0 and on["prob"]:
                        if loop or n >= 3:
                            pe.wait_ge(attn_copied, s.plus(-3).times(1, 1))
                        else:
                            pe.wait_ge(max_copied, s.plus(-1).times(2, 1))
                        turn_max(s.plus(-1), 1)
                    if g == 0 and on["proj"]:
                        if n == 1:
                            pe.wait_ge(x_t_loaded[1], 16)
                        if on["prob"]:
                            pe.wait_ge(max_copied, s.plus(-1).times(2, 2))
                        else:
                            pe.wait_ge(part_rest, 1)
                        project_qk(s.plus(1))
                    if g == 1 and on["score"]:
                        if loop or n >= 3:
                            pe.wait_ge(resid_done, s.plus(-3).times(1, 1))
                            pe.wait_ge(logits_copied, s.plus(-3).times(1, HEAD))
                        elif n >= 1:
                            pe.wait_ge(v_padded, s.plus(-1).times(4, 4))
                        project_v(s)
                    if g == 1 and on["tail"]:
                        if on["score"]:
                            pe.wait_ge(v_padded, s.times(4, 4))
                        else:
                            pe.wait_ge(resid_done, s.plus(-3).times(1, 1))
                            pe.wait_ge(logits_copied, s.plus(-3).times(1, HEAD))
                        turn_output(s.plus(-2))
                    if g == 2 and on["score"]:
                        if on["proj"]:
                            pe.wait_ge(part_rest, s.plus(1).times(1, 1))
                        else:
                            pe.wait_ge(max_copied, s.plus(-1).times(2, 2))
                        turn_max(s, 0)
                    if g == 2 and on["tail"]:
                        if on["score"]:
                            pe.wait_ge(max_copied, s.times(2, 1))
                        elif on["prob"]:
                            pe.wait_ge(max_copied, s.plus(-1).times(2, 2))
                        else:
                            pe.wait_ge(attn_copied, s.plus(-3).times(1, 1))
                        turn_attention(s.plus(-2))
                    if g == 2 and on["turn"]:
                        if on["tail"]:
                            pe.wait_ge(normed, s.plus(-2).times(4, 4))
                        else:
                            pe.wait_ge(resid_done, s.plus(-3).times(1, 1))
                            pe.wait_ge(logits_copied, s.plus(-3).times(1, HEAD))
                        turn_x1(s.plus(-3))
                    if g == 3 and on["tail"]:
                        if on["turn"]:
                            pe.wait_ge(x1_copied, s.plus(-3).times(1, 1))
                        else:
                            pe.wait_ge(normed, s.plus(-2).times(4, 4))
                        project_out(s.plus(-2))
                    if g == 3 and on["turn"]:
                        if on["tail"]:
                            pe.wait_ge(resid_done, s.plus(-2).times(1, 1))
                        route_logits(s.plus(-3))

            pe.wait_ge(moe_w_loaded, 16 * 5)
            all_steps(pe, step)

            def first_layer(c, e):
                if e >= 2:
                    pe.wait_ge(gelu_done, c * NX + (HEAD + e - 1))
                else:
                    pe.wait_ge(gelu_done, c * NX + HEAD)
                cols = bass.ds(c * CH, CH)
                for i, (w, xx) in enumerate(((w_in_lo, x1_hi), (w_in_hi, x1_lo), (w_in_hi, x1_hi))):
                    last = mm(bank[e % 2][:, :], w[:, e, :], xx[:, cols], start=i == 0, stop=i == 2)
                last.then_inc(hid_ready, 1)

            def second_layer(c, e):
                pe.wait_ge(gelu_done, c * NX + (HEAD + e + 1))
                if e >= 2:
                    pe.wait_ge(y_added, c * (NX * CT) + (HEAD + (e - 1) * CT))
                else:
                    pe.wait_ge(y_added, c * (NX * CT) + HEAD)
                for n in range(CT):
                    last = mm(bank[2 + e % 2][:, n * E:(n + 1) * E], hid[e % 2][:, n * P:(n + 1) * P], w_out_sb[:, e, :], start=True, stop=True)
                last.then_inc(y_ready, 1)

            pe.wait_ge(w_lo_done, 1)
            pe.wait_ge(x1_lo_done, HEAD + B)
            with pe.Fori(0, NCH) as c:
                first_layer(c, 0)
                pe.wait_ge(gate_staged, c + 1)
                for n in range(CT):
                    last = nc.tensor.transpose(bank[4][0:NX, n * P:(n + 1) * P], gate_c[:, n, :], ident[:, :])
                last.then_inc(gate_turned, 1)
                first_layer(c, 1)
                pe.wait_ge(gate_copied, c + 1)
                for n in range(CT):
                    last = mm(bank[5][:, n * E:(n + 1) * E], gate_t[:, n * P:(n + 1) * P], b_out_sb[:, :], start=True, stop=True)
                last.then_inc(bias_ready, 1)
                second_layer(c, 0)
                for e in range(2, NX):
                    first_layer(c, e)
                    second_layer(c, e - 1)
                second_layer(c, NX - 1)


_OUT = (B, T, E)


def kernel(L0_attn_x, L0_attn_w_qkv, L0_attn_w_out, L0_ffn_router_w, L0_ffn_w_in, L0_ffn_b_in, L0_ffn_w_out, L0_ffn_b_out):
    import numpy as np
    import concourse.bacc as bacc
    from concourse.bass_utils import run_bass_kernel_spmd

    x = np.asarray(L0_attn_x)
    tokens = x.reshape(B * T, E)
    wqkv = np.asarray(L0_attn_w_qkv)
    by_dim = (np.arange(E) % H) * D + np.arange(E) // H
    wq, wk, wv = wqkv[0:E][by_dim], wqkv[E:2 * E][by_dim], wqkv[2 * E:3 * E]
    arrays = {
        "x_t": tokens.T,
        "x": tokens,
        "wqkv_t": np.concatenate([wq, wk, wv], 0).T,
        "wout_t": np.asarray(L0_attn_w_out).T,
        "router_w": np.asarray(L0_ffn_router_w),
        "w_in": np.asarray(L0_ffn_w_in),
        "b_in_t": np.asarray(L0_ffn_b_in).T,
        "w_out": np.asarray(L0_ffn_w_out),
        "b_out": np.asarray(L0_ffn_b_out),
    }
    arrays = {name: np.ascontiguousarray(a) for name, a in arrays.items()}
    nc = bacc.Bacc("TRN2", target_bir_lowering=False, num_devices=1)
    args = [nc.dram_tensor(name, a.shape, F32, kind="ExternalInput").ap() for name, a in arrays.items()]
    args.append(nc.dram_tensor("out", (B * T, E), F32, kind="ExternalOutput").ap())
    attention_moe(nc, *args)
    r = run_bass_kernel_spmd(nc, [arrays], core_ids=[0])
    return r.results[0]["out"].reshape(_OUT)
```

```python
import concourse.bass as bass
from concourse import mybir
from contextlib import ExitStack

F32 = mybir.dt.float32
F32R = mybir.dt.float32r
BF16 = mybir.dt.bfloat16
ALU = mybir.AluOpType
ACT = mybir.ActivationFunctionType
X_AXIS = mybir.AxisListType.X

P = 128
B = 8
T = 256
E = 128
H = 16
D = E // H
W = 128
NX = 8
PARTS = 3
BLK = PARTS * D
ROWS = PARTS * BLK
KROWS = ROWS + PARTS
QUADS = H // 4
HALF = H // 2
TILES = B * T // P
CH = 512
CT = CH // P
NCH = B * T // CH
VW = 32
SCALE = 1.0 / float(D) ** 0.5
EPS = 1e-5
GATES_AFTER = 5
MASKED = -(2.0 ** 100)
HEAD = 1


class Batch:

    def __init__(self, pair, parity):
        self.pair, self.parity = pair, parity

    def plus(self, k):
        t = self.parity + k
        return Batch(self.pair + t // 2, t % 2)

    def times(self, per, more=0):
        return self.pair * (2 * per) + (per * self.parity + more)


def wait_apart(engine, semaphore, value, passed):
    engine.wait_ge(semaphore, value)
    engine.sem_inc(passed, 1)


def attention_moe(nc, x_t, x, wqkv_t, wout_t, router_w, w_in, b_in_t, w_out, b_out, out):
    q_scratch = nc.dram_tensor("q_scratch", [2 * PARTS * E, T], BF16, kind="Internal").ap()
    k_scratch = nc.dram_tensor("k_scratch", [2 * (2 * PARTS - 1) * E, T], BF16, kind="Internal").ap()

    with ExitStack() as ctx:
        def sb(name, shape, dt=F32):
            return ctx.enter_context(nc.sbuf_tensor(name, shape, dt))

        def sem(name):
            return ctx.enter_context(nc.semaphore(name))

        bank = [ctx.enter_context(nc.psum_tensor(f"bank{i}", [P, 512], F32)) for i in range(8)]
        score_bank, st_bank, o_bank = bank[0:3], bank[3:5], bank[5]
        misc = bank[6:8]
        y_bank = [bank[2], bank[3], bank[5], bank[6]]
        gate_bank, bias_bank = bank[4], bank[7]

        ident = sb("ident", [P, P])
        ident_bf = sb("ident_bf", [P, P], BF16)
        mask_first = sb("mask_first", [P, P], BF16)
        mask_second = sb("mask_second", [P, 2, 64], BF16)
        half_power = sb("half_power", [P, CT])
        wqkv_sb = sb("wqkv_sb", [P, 3 * E])
        wout_sb = sb("wout_sb", [P, E])
        router_sb = sb("router_sb", [P, NX])
        b_in_sb = sb("b_in_sb", [P, NX])
        b_out_sb = sb("b_out_sb", [NX, E])
        w_in_sb = sb("w_in_sb", [P, NX, P])
        w_in_hi = sb("w_in_hi", [P, NX, P], F32R)
        w_in_lo = sb("w_in_lo", [P, NX, P], F32R)
        w_out_sb = sb("w_out_sb", [P, NX, E])
        x_t_sb = sb("x_t_sb", [P, B * T])
        xt_sb = [sb(f"x_cols{i}", [P, T]) for i in range(2)]
        x_sb = [sb(f"x_rows{i}", [P, 2, E]) for i in range(2)]
        parts = [sb(f"parts{i}", [P, PARTS, 2, T], BF16) for i in range(2)]
        rest = sb("rest", [P, 2, T])
        qs = [[sb(f"qs{i}{h}", [P, HALF, T], BF16) for h in range(2)] for i in range(2)]
        ks = [[sb(f"ks{i}{h}", [P, HALF, T], BF16) for h in range(2)] for i in range(2)]
        v_sb = [sb(f"v{i}", [P, 2, H, VW]) for i in range(2)]
        neg_max = sb("neg_max", [P, 2, H])
        max_rest = sb("max_rest", [P, 2, HALF])
        max_parts = sb("max_parts", [P, 2, PARTS, HALF], BF16)
        max_t = [sb(f"max_t{h}", [PARTS * HALF, T], BF16) for h in range(2)]
        probs = [sb(f"probs{g}", [P, 3, 4, P]) for g in range(QUADS)]
        o_t = sb("o_t", [P, 2, T])
        inv_sum = sb("inv_sum", [P, 2, H])
        attn = sb("attn", [P, 2, E])
        attn_t = sb("attn_t", [P, T])
        resid = sb("resid", [P, 2, E])
        stats = sb("stats", [P, 2, 6])
        moments = sb("moments", [P, 2, 2])
        var_eps = sb("var_eps", [P, 2])
        rstd = sb("rstd", [P, 2])
        x1 = sb("x1_rows", [P, TILES, E])
        x1_pair = sb("x1_pair", [P, 2, E])
        x1_t = sb("x1_t", [P, T])
        x1_hi = sb("x1_hi", [P, B * T], F32R)
        x1_lo = sb("x1_lo", [P, B * T], F32R)
        logits = sb("logits", [P, TILES, NX])
        route = [sb(f"route{i}", [P, TILES, NX]) for i in range(6)]
        row_stat = [sb(f"row_stat{i}", [P, TILES]) for i in range(6)]
        rank_w = sb("rank_w", [P, TILES, NX])
        gate = sb("gate", [P, TILES, NX])
        gate_c = sb("gate_c", [P, CT, NX])
        gate_t = sb("gate_t", [NX, CH])
        hid = [sb(f"hid{i}", [P, CH]) for i in range(2)]
        acc = sb("acc", [P, CT, E])
        stats2 = sb("stats2", [P, CT, 6])
        moments2 = sb("moments2", [P, CT, 2])
        var2 = sb("var2", [P, CT])
        rstd2 = sb("rstd2", [P, CT])
        y_sb = sb("y_sb", [P, CT, E])

        qkv_w_loaded, out_w_loaded, moe_w_loaded = sem("qkv_w_loaded"), sem("out_w_loaded"), sem("moe_w_loaded")
        x_t_loaded = [sem(f"x_t_loaded{i}") for i in range(2)]
        xt_loaded = [sem(f"xt_loaded{i}") for i in range(2)]
        x_loaded = [sem(f"x_loaded{i}") for i in range(2)]
        consts_ready = sem("consts_ready")
        sp_passed, pool_passed, dve_passed = sem("sp_passed"), sem("pool_passed"), sem("dve_passed")
        base_ready, ones_ready = sem("base_ready"), sem("ones_ready")
        v_zeroed, v_ones = sem("v_zeroed"), sem("v_ones")
        maxima, x1_kept = sem("maxima"), sem("x1_kept")
        qk_projected, v_projected = sem("qk_projected"), sem("v_projected")
        part_top, part_rest, part_mid, part_low = sem("part_top"), sem("part_rest"), sem("part_mid"), sem("part_low")
        scratch_written = [sem(f"scratch_written{i}") for i in range(2)]
        stacked = [[sem(f"stacked{i}{h}") for h in range(2)] for i in range(2)]
        v_padded = sem("v_padded")
        scores_ready = sem("scores_ready")
        max_top, max_rested, max_mid, max_split = sem("max_top"), sem("max_rested"), sem("max_mid"), sem("max_split")
        max_turned, max_copied = sem("max_turned"), sem("max_copied")
        max_stacked = [[sem(f"max_stacked{i}{h}") for h in range(2)] for i in range(2)]
        st_ready, exp_done, masked, pv_done = sem("st_ready"), sem("exp_done"), sem("masked"), sem("pv_done")
        o_copied, o_turned, sums_inverted, normed = sem("o_copied"), sem("o_turned"), sem("sums_inverted"), sem("normed")
        attn_turned, attn_copied, projected = sem("attn_turned"), sem("attn_copied"), sem("projected")
        resid_done, stats_done, moments_done = sem("resid_done"), sem("stats_done"), sem("moments_done")
        eps_added, rstd_done, x1_done = sem("eps_added"), sem("rstd_done"), sem("x1_done")
        x1_turned, x1_copied, x1_hi_done, x1_lo_done = sem("x1_turned"), sem("x1_copied"), sem("x1_hi_done"), sem("x1_lo_done")
        logits_ready, logits_copied = sem("logits_ready"), sem("logits_copied")
        w_hi_done, w_lo_done = sem("w_hi_done"), sem("w_lo_done")
        routing, route_shifted, route_exp, gate_done = sem("routing"), sem("route_shifted"), sem("route_exp"), sem("gate_done")
        rank_ready = sem("rank_ready")
        gate_staged, gate_turned, gate_copied, bias_ready = sem("gate_staged"), sem("gate_turned"), sem("gate_copied"), sem("bias_ready")
        hid_ready, gelu_done, y_ready, y_added = sem("hid_ready"), sem("gelu_done"), sem("y_ready"), sem("y_added")
        bias_added, stats2_done, moments2_done = sem("bias_added"), sem("stats2_done"), sem("moments2_done")
        eps2_added, rstd2_done, y_normed, stored = sem("eps2_added"), sem("rstd2_done"), sem("y_normed"), sem("stored")

        block = ctx.enter_context(nc.Block())

        FULL = dict(proj=True, score=True, prob=True, tail=True, turn=True, pv_last=True)
        STEPS_BEFORE = [
            (0, dict(FULL, prob=False, tail=False, turn=False, pv_last=False)),
            (1, dict(FULL, tail=False, turn=False, pv_last=False)),
            (2, dict(FULL, turn=False)),
        ]
        LOOP_STEPS = (3, 7)
        STEPS_AFTER = [
            (7, dict(FULL, proj=False)),
            (8, dict(FULL, proj=False, score=False)),
            (9, dict(FULL, proj=False, score=False, prob=False)),
            (10, dict(FULL, proj=False, score=False, prob=False, tail=False, pv_last=False)),
        ]

        def all_steps(engine, step):
            for s, on in STEPS_BEFORE:
                step(Batch(s // 2, s % 2), on, s)
            with engine.Fori(LOOP_STEPS[0] // 2, LOOP_STEPS[1] // 2) as pair:
                step(Batch(pair, 1), FULL, None)
                step(Batch(pair, 1).plus(1), FULL, None)
            for s, on in STEPS_AFTER:
                step(Batch(s // 2, s % 2), on, s)

        @block.sync
        def _(sp):
            def load_xt(b):
                sp.dma_start(xt_sb[b.parity][:, :], x_t[:, bass.ds(b.times(T), T)]).then_inc(xt_loaded[b.parity], 16)

            def load_x(b):
                sp.dma_start(x_sb[b.parity][:, :, :],
                             x[bass.ds(b.times(T), T), :].rearrange("(n p) e -> p n e", p=P)) \
                    .then_inc(x_loaded[b.parity], 16)

            def write_parts(b):
                par = b.parity
                q0, k0 = par * PARTS * E, par * (2 * PARTS - 1) * E
                sp.wait_ge(part_low, b.times(1, 1))
                sp.dma_start(q_scratch[q0:q0 + PARTS * E, :].rearrange("(a r) t -> r a t", a=PARTS),
                             parts[par][:, :, 0, :]).then_inc(scratch_written[par], 16)
                sp.dma_start(k_scratch[k0:k0 + PARTS * E, :].rearrange("(a r) t -> r a t", a=PARTS),
                             parts[par][:, :, 1, :]).then_inc(scratch_written[par], 16)
                sp.dma_start(k_scratch[k0 + PARTS * E:k0 + (2 * PARTS - 1) * E, :]
                             .rearrange("(a r) t -> r a t", a=PARTS - 1),
                             parts[par][:, 0:PARTS - 1, 1, :]).then_inc(scratch_written[par], 16)
                wait_apart(sp, scratch_written[par], b.pair * 48 + 48, sp_passed)

            def stack(b, h, in_use):
                par = b.parity
                if in_use:
                    sp.wait_ge(st_ready, b.plus(-2).times(H, HALF * (h + 1)))
                for scratch, operand, copies, step_r in ((q_scratch, qs, PARTS, 0), (k_scratch, ks, 2 * PARTS - 1, D * H * T)):
                    at = par * copies * E * T + h * HALF * T
                    sp.dma_start(operand[par][h][0:ROWS, :, :],
                                 bass.AP(scratch.tensor, scratch.offset + at, [[step_r, PARTS], [H * T, BLK], [1, HALF * T]])) \
                        .then_inc(stacked[par][h], 16)

            def stack_max(b, h):
                sp.wait_ge(max_copied, b.times(2, h + 1))
                sp.dma_start(qs[b.parity][h][ROWS:KROWS, :, :], max_t[h][:, :]).then_inc(max_stacked[b.parity][h], 16)

            b0, b1 = Batch(0, 0), Batch(0, 1)
            sp.dma_start(wqkv_sb[:, :], wqkv_t).then_inc(qkv_w_loaded, 16)
            sp.dma_start(x_t_sb[:, 0:2 * T], x_t[:, 0:2 * T]).then_inc(x_t_loaded[0], 16)
            load_xt(b0)
            sp.dma_start(wout_sb[:, :], wout_t).then_inc(out_w_loaded, 16)
            load_x(b0)
            load_x(b1)
            sp.dma_start(router_sb[:, :], router_w).then_inc(moe_w_loaded, 16)
            sp.dma_start(b_in_sb[:, :], b_in_t).then_inc(moe_w_loaded, 16)
            sp.dma_start(b_out_sb[:, :], b_out).then_inc(moe_w_loaded, 16)
            sp.dma_start(x_t_sb[:, 2 * T:B * T], x_t[:, 2 * T:B * T]).then_inc(x_t_loaded[1], 16)
            sp.wait_ge(ones_ready, 2)
            write_parts(b0)
            stack(b0, 0, False)
            stack(b0, 1, False)
            sp.dma_start(w_in_sb[:, :, :], w_in.rearrange("e d h -> d e h")).then_inc(moe_w_loaded, 16)
            sp.dma_start(w_out_sb[:, :, :], w_out.rearrange("e h d -> h e d")).then_inc(moe_w_loaded, 16)

            def step(s, on, n):
                if n is None or 3 <= n <= B:
                    wait_apart(sp, resid_done, s.plus(-3).times(1, 1), sp_passed)
                    load_x(s.plus(-1))
                if on["prob"]:
                    stack_max(s.plus(-1), 1)
                if on["proj"]:
                    if n is None or n >= 1:
                        wait_apart(sp, v_projected, s.plus(-1).times(1, 1), sp_passed)
                    load_xt(s.plus(1))
                if on["proj"]:
                    write_parts(s.plus(1))
                    stack(s.plus(1), 0, n is None or n >= 1)
                if on["score"]:
                    stack_max(s, 0)
                if on["proj"]:
                    stack(s.plus(1), 1, n is None or n >= 1)

            all_steps(sp, step)
            with sp.Fori(0, NCH) as c:
                wait_apart(sp, y_normed, c * CT + CT, sp_passed)
                sp.dma_start(out[bass.ds(c * CH, CH), :].rearrange("(n p) e -> p n e", p=P), y_sb[:, :, :]) \
                    .then_inc(stored, 16)
            sp.wait_ge(stored, NCH * 16)

        @block.gpsimd
        def _(pool):
            pool.sem_inc(x1_kept, HEAD)
            pool.memset(ident[:, :], 0.0).then_inc(base_ready, 1)
            pool.memset(ident_bf[:, :], 0.0).then_inc(base_ready, 1)
            pool.memset(mask_first[:, :], 0.0).then_inc(base_ready, 1)
            pool.memset(mask_second[:, :, :], 0.0).then_inc(base_ready, 1)
            pool.memset(half_power[:, :], -0.5).then_inc(base_ready, 1)
            pool.wait_ge(base_ready, 5)
            for m in (ident, ident_bf):
                pool.affine_select(out=m[:, :], in_=m[:, :], compare_op=ALU.not_equal, fill=1.0, base=0,
                                   pattern=[[-1, P]], channel_multiplier=1).then_inc(consts_ready, 1)
            pool.affine_select(out=mask_first[:, :], in_=mask_first[:, :], compare_op=ALU.is_ge, fill=MASKED, base=0,
                               pattern=[[-1, P]], channel_multiplier=1).then_inc(consts_ready, 1)
            for lo in (0, 64):
                pool.wait_ge(consts_ready, 3 + lo // 32)
                part = mask_second[lo:lo + 64, 0, :]
                pool.affine_select(out=part, in_=part, compare_op=ALU.is_gt, fill=MASKED, base=0,
                                   pattern=[[1, 64]], channel_multiplier=-1).then_inc(consts_ready, 1)
                part = mask_second[lo:lo + 64, 1, :]
                pool.affine_select(out=part, in_=part, compare_op=ALU.is_ge, fill=MASKED, base=0,
                                   pattern=[[-1, 64]], channel_multiplier=1).then_inc(consts_ready, 1)
            pool.wait_ge(consts_ready, 7)
            for par in range(2):
                pool.memset(v_sb[par][:, :, :, :], 0.0).then_inc(v_zeroed, 1)
            pool.wait_ge(v_zeroed, 2)
            for par in range(2):
                for kt in range(2):
                    for s in range(2):
                        ones = v_sb[par][:, kt, :, :].rearrange("p (t s j) c -> p t s j c", t=2, s=2)[:, :, s, :, (D + 1) * s + D]
                        pool.memset(ones, 1.0).then_inc(v_ones, 1)
            for e in range(NX):
                pool.memset(rank_w[:, :, e:e + 1], float(NX - e)).then_inc(rank_ready, 1)

            def step(s, on, n):
                if on["turn"]:
                    b = s.plus(-3)
                    wait_apart(pool, moments_done, b.times(2, 2), pool_passed)
                    pool.tensor_scalar(var_eps[:, :], moments[:, :, 1], EPS, None, ALU.add).then_inc(eps_added, 1)
                    pool.wait_ge(eps_added, b.times(1, 1))
                    pool.tensor_tensor(rstd[:, :], var_eps[:, :], half_power[:, 0:2], ALU.pow).then_inc(rstd_done, 1)
                for g in range(QUADS):
                    if on["prob"]:
                        b = s.plus(-1)
                        wait_apart(pool, exp_done, b.times(H, 4 * g + 4), pool_passed)
                        own, other = probs[g][:, 0:3:2, :, :], probs[g][:, 1, :, :]
                        pool.affine_select(out=own, in_=own, compare_op=ALU.is_ge,
                                           fill=0.0, base=0, pattern=[[0, 2], [0, 4], [1, P]],
                                           channel_multiplier=-1).then_inc(masked, 1)
                        pool.affine_select(out=other, in_=other, compare_op=ALU.is_gt,
                                           fill=0.0, base=0, pattern=[[0, 4], [-1, P]],
                                           channel_multiplier=1).then_inc(masked, 1)
                    if g == 1 and on["turn"]:
                        b = s.plus(-3)
                        pool.wait_ge(x1_done, b.times(2, 2))
                        pool.tensor_copy(x1[:, bass.ds(b.times(2), 2), :], x1_pair[:, :, :]).then_inc(x1_kept, 1)

            all_steps(pool, step)
            with pool.Fori(0, NCH) as c:
                wait_apart(pool, moments2_done, c * CT + CT, pool_passed)
                pool.tensor_scalar(var2[:, :], moments2[:, :, 1], EPS, None, ALU.add).then_inc(eps2_added, 1)
                pool.wait_ge(eps2_added, c + 1)
                pool.tensor_tensor(rstd2[:, :], var2[:, :], half_power[:, :], ALU.pow).then_inc(rstd2_done, 1)

        @block.scalar
        def _(act):
            def exponentials(b, g, i, in_use):
                k = 4 * g + i
                if i == 0 and in_use:
                    act.wait_ge(pv_done, b.plus(-1).times(QUADS, g + 1))
                act.wait_ge(st_ready, b.times(H, k + 1))
                nc.scalar.activation(probs[g][:, :, i, :], st_bank[k % 2][:, 0:3 * P].rearrange("p (k c) -> p k c", k=3), ACT.Exp, scale=SCALE) \
                    .then_inc(exp_done, 1)

            def copy_max(b, h, in_use):
                act.wait_ge(max_turned, b.times(2, h + 1))
                if in_use:
                    act.wait_ge(max_stacked[b.plus(-1).parity][h], b.plus(-1).pair * 16 + 16)
                nc.scalar.activation(max_t[h][:, :], misc[0][0:PARTS * HALF, :].bitcast(BF16)[:, 0:T], ACT.Copy).then_inc(max_copied, 1)

            def step(s, on, n):
                for g in range(QUADS):
                    for i in range(4):
                        if on["prob"]:
                            exponentials(s.plus(-1), g, i, n is None or n >= 2)
                        if (g, i) == (0, 1) and on["proj"]:
                            take_top(s.plus(1), n is None or n >= 1)
                        if (g, i) == (1, 1) and on["score"]:
                            pad_v(s, n is None or n >= 2)
                        if (g, i) == (3, 1) and on["tail"]:
                            act.wait_ge(attn_turned, s.plus(-2).times(1, 1))
                            if n is None or n >= 3:
                                act.wait_ge(projected, s.plus(-3).times(1, 1))
                            nc.scalar.activation(attn_t[:, :], misc[0][:, 0:T], ACT.Copy).then_inc(attn_copied, 1)
                        if (g, i) == (2, 2) and on["score"]:
                            copy_max(s, 0, n is None or n >= 1)
                        if (g, i) == (3, 2) and on["turn"]:
                            b = s.plus(-3)
                            act.wait_ge(logits_ready, b.times(1, HEAD + 1))
                            nc.scalar.activation(logits[:, bass.ds(b.times(2), 2), :],
                                                 misc[1][:, 0:2 * NX].rearrange("p (n e) -> p n e", n=2), ACT.Copy).then_inc(logits_copied, 1)
                    if g == 0 and on["pv_last"]:
                        b = s.plus(-2)
                        act.wait_ge(pv_done, b.times(QUADS, QUADS))
                        if n is None or n >= 3:
                            act.wait_ge(o_turned, b.plus(-1).times(1, 1))
                        nc.scalar.activation(o_t[:, :, :], o_bank[:, :].rearrange("p (t q) -> p t q", t=2), ACT.Copy).then_inc(o_copied, 1)
                    if g == 0 and on["prob"]:
                        copy_max(s.plus(-1), 1, n is None or n >= 2)
                    if g == 2 and on["turn"]:
                        b = s.plus(-3)
                        act.wait_ge(x1_turned, b.times(1, HEAD + 1))
                        if n is None or n >= 4:
                            act.wait_ge(x1_lo_done, b.times(1, HEAD))
                            act.wait_ge(logits_ready, b.times(1, HEAD))
                        nc.scalar.activation(x1_t[:, :], misc[1][:, 0:T], ACT.Copy).then_inc(x1_copied, 1)

            def take_top(b, in_use):
                act.wait_ge(qk_projected, b.times(1, 1))
                if in_use:
                    act.wait_ge(scratch_written[b.parity], b.plus(-2).pair * 48 + 48)
                nc.scalar.activation(parts[b.parity][:, 0, :, :], misc[0][:, :].rearrange("p (a t) -> p a t", a=2), ACT.Copy).then_inc(part_top, 1)

            def pad_v(b, in_use):
                act.wait_ge(v_projected, b.times(1, 1))
                if in_use:
                    act.wait_ge(pv_done, b.plus(-2).times(QUADS, QUADS))
                else:
                    act.wait_ge(v_ones, 8)
                for kt in range(2):
                    for s in range(2):
                        dst = v_sb[b.parity][:, kt, :, (D + 1) * s:(D + 1) * s + D].rearrange("p (t s j) c -> p t s j c", t=2, s=2)[:, :, s, :, :]
                        src = misc[1][:, kt * E:(kt + 1) * E].rearrange("p (t s j c) -> p t s j c", t=2, s=2, j=4)[:, :, s, :, :]
                        nc.scalar.activation(dst, src, ACT.Copy).then_inc(v_padded, 1)

            act.sem_inc(logits_copied, HEAD)
            take_top(Batch(0, 0), False)
            all_steps(act, step)

            act.wait_ge(route_shifted, 1)
            nc.scalar.activation(route[1][:, :, :], route[0][:, :, :], ACT.Exp).then_inc(route_exp, 1)
            def chunk(c, first):
                for e in range(NX):
                    act.wait_ge(hid_ready, c * NX + (e + 1))
                    if e >= 2 or not first:
                        act.wait_ge(y_ready, c * NX + (e - 1))
                    nc.scalar.activation(hid[e % 2][:, :], bank[e % 2][:, :], ACT.Gelu_apprx_tanh,
                                         bias=b_in_sb[:, e:e + 1]).then_inc(gelu_done, 1)
                    if e == GATES_AFTER:
                        act.wait_ge(gate_turned, c + 1)
                        nc.scalar.activation(gate_t[:, :], gate_bank[0:NX, :], ACT.Copy).then_inc(gate_copied, 1)

            chunk(0, True)
            with act.Fori(1, NCH) as c:
                chunk(c, False)

        @block.vector
        def _(dve):
            def split_rest(b):
                p = parts[b.parity]
                dve.wait_ge(part_top, b.times(1, 1))
                nc.vector.tensor_tensor(rest[:, :, :], misc[0][:, :].rearrange("p (a t) -> p a t", a=2), p[:, 0, :, :],
                                        ALU.subtract).then_inc(part_rest, 1)
                dve.wait_ge(part_rest, b.times(1, 1))
                nc.vector.tensor_copy(p[:, 1, :, :], rest[:, :, :]).then_inc(part_mid, 1)
                dve.wait_ge(part_mid, b.times(1, 1))
                nc.vector.tensor_tensor(p[:, 2, :, :], rest[:, :, :], p[:, 1, :, :], ALU.subtract).then_inc(part_low, 1)

            def split_max(b, h, in_use):
                full = neg_max[:, :, h * HALF:(h + 1) * HALF]
                k = b.times(2, h + 1)
                dve.wait_ge(maxima, b.times(3 * QUADS, 3 * (QUADS // 2) * (h + 1)))
                if in_use:
                    dve.wait_ge(max_turned, b.times(2, h))
                nc.vector.tensor_copy(max_parts[:, :, 0, :], full).then_inc(max_top, 1)
                dve.wait_ge(max_top, k)
                nc.vector.tensor_tensor(max_rest[:, :, :], full, max_parts[:, :, 0, :], ALU.subtract).then_inc(max_rested, 1)
                dve.wait_ge(max_rested, k)
                nc.vector.tensor_copy(max_parts[:, :, 1, :], max_rest[:, :, :]).then_inc(max_mid, 1)
                dve.wait_ge(max_mid, k)
                nc.vector.tensor_tensor(max_parts[:, :, 2, :], max_rest[:, :, :], max_parts[:, :, 1, :], ALU.subtract).then_inc(max_split, 1)

            def normalise(b):
                turned = misc[1][:, :].rearrange("p (n t j c) -> p n t j c", n=2, t=2, j=4)
                dve.wait_ge(o_turned, b.times(1, 1))
                for n in range(2):
                    nc.vector.reciprocal(inv_sum[:, n, :].rearrange("p (t s j) -> p t j s", t=2, s=2),
                                         turned[:, n, :, :, D:2 * (D + 1):D + 1]).then_inc(sums_inverted, 1)
                dve.wait_ge(sums_inverted, b.times(2, 2))
                for n in range(2):
                    for t in range(2):
                        src = turned[:, n, t, :, 0:2 * (D + 1)].rearrange("p j (s c) -> p s j c", s=2)[:, :, :, 0:D]
                        inv = inv_sum[:, n, t * HALF:(t + 1) * HALF].rearrange("p (s j) -> p s j", s=2).unsqueeze(3).to_broadcast([P, 2, 4, D])
                        dst = attn[:, n, t * 64:(t + 1) * 64].rearrange("p (s j c) -> p s j c", s=2, j=4)
                        nc.vector.tensor_tensor(dst, src, inv, ALU.mult).then_inc(normed, 1)

            def first_residual(b):
                dve.wait_ge(projected, b.times(1, 1))
                dve.wait_ge(x_loaded[b.parity], b.pair * 16 + 16)
                nc.vector.tensor_tensor(resid[:, :, :], misc[1][:, 0:T].rearrange("p (n e) -> p n e", n=2),
                                        x_sb[b.parity][:, :, :], ALU.add).then_inc(resid_done, 1)

            def first_stats(b):
                dve.wait_ge(resid_done, b.times(1, 1))
                for n in range(2):
                    nc.vector.bn_stats(stats[:, n, :], resid[:, n, :]).then_inc(stats_done, 1)

            def first_moments(b):
                wait_apart(dve, stats_done, b.times(2, 2), dve_passed)
                for n in range(2):
                    nc.vector.bn_aggr(moments[:, n, :], stats[:, n, :]).then_inc(moments_done, 1)

            def first_norm(b, in_use):
                dve.wait_ge(rstd_done, b.times(1, 1))
                if in_use:
                    dve.wait_ge(x1_kept, b.times(1, HEAD))
                    dve.wait_ge(x1_turned, b.times(1, HEAD))
                for n in range(2):
                    nc.vector.tensor_scalar(x1_pair[:, n, :], resid[:, n, :], moments[:, n, 0:1], rstd[:, n:n + 1],
                                            ALU.subtract, ALU.mult).then_inc(x1_done, 1)

            def split_x1(b):
                cols = bass.ds(b.times(T), T)
                dve.wait_ge(x1_copied, b.times(1, 1))
                nc.vector.tensor_copy(x1_hi[:, cols], x1_t[:, :]).then_inc(x1_hi_done, 1)
                dve.wait_ge(x1_hi_done, b.times(1, 1))
                nc.vector.tensor_tensor(x1_lo[:, cols], x1_t[:, :], x1_hi[:, cols].bitcast(F32), ALU.subtract).then_inc(x1_lo_done, 1)

            def max_first_tile(s, g):
                dve.wait_ge(scores_ready, s.times(3 * QUADS, 3 * g + 1))
                nc.vector.tensor_reduce(neg_max[:, 0, 4 * g:4 * g + 4], score_bank[0][:, :].rearrange("p (h c) -> p h c", h=4),
                                        X_AXIS, ALU.max, negate=True).then_inc(maxima, 1)

            def max_second_tile(s, g, u):
                dve.wait_ge(scores_ready, s.times(3 * QUADS, 3 * g + 2 + u))
                nc.vector.tensor_reduce(neg_max[:, 1, 4 * g + 2 * u:4 * g + 2 * u + 2],
                                        score_bank[1 + u][:, 0:384].rearrange("p (h c) -> p h c", h=2),
                                        X_AXIS, ALU.max, negate=True).then_inc(maxima, 1)

            def step(s, on, n):
                for g in range(QUADS):
                    if g == 0 and on["turn"]:
                        first_residual(s.plus(-3))
                    if g == 1 and on["turn"]:
                        first_norm(s.plus(-3), n is None or n >= 4)
                    if on["score"]:
                        if g == 0 and (n is None or n >= 1):
                            dve.wait_ge(max_split, s.plus(-1).times(2, 2))
                        max_first_tile(s, g)
                    if g == 0 and on["turn"]:
                        first_stats(s.plus(-3))
                    if g == 2 and on["tail"]:
                        normalise(s.plus(-2))
                    if g == 3 and on["turn"]:
                        split_x1(s.plus(-3))
                    if on["score"]:
                        max_second_tile(s, g, 0)
                    if g == 0 and on["turn"]:
                        first_moments(s.plus(-3))
                    if on["score"]:
                        max_second_tile(s, g, 1)
                        if g == 1:
                            split_max(s, 0, n is None or n >= 1)
                        if g == 3:
                            split_max(s, 1, True)
                    if g == 0 and on["proj"]:
                        split_rest(s.plus(1))
                if n == 1:
                    dve.wait_ge(moe_w_loaded, 16 * 5)
                    nc.vector.tensor_copy(w_in_hi[:, :, :], w_in_sb[:, :, :]).then_inc(w_hi_done, 1)
                    dve.wait_ge(w_hi_done, 1)
                    nc.vector.tensor_tensor(w_in_lo[:, :, :], w_in_sb[:, :, :], w_in_hi[:, :, :].bitcast(F32), ALU.subtract).then_inc(w_lo_done, 1)

            dve.sem_inc(x1_lo_done, HEAD)
            for par in range(2):
                for h in range(2):
                    nc.vector.memset(ks[par][h][64:P, :, :], 1.0).then_inc(ones_ready, 1)
                if par == 0:
                    split_rest(Batch(0, 0))
            all_steps(dve, step)

            links = 0

            def link(ins):
                nonlocal links
                links += 1
                ins.then_inc(routing, 1)
                dve.wait_ge(routing, links)

            def wide(ap):
                return ap[:, :].unsqueeze(2).to_broadcast([P, TILES, NX])

            dve.wait_ge(logits_copied, HEAD + B)
            link(nc.vector.tensor_reduce(row_stat[0][:, :], logits[:, :, :], X_AXIS, ALU.max))
            nc.vector.tensor_tensor(route[0][:, :, :], logits[:, :, :], wide(row_stat[0]), ALU.subtract).then_inc(route_shifted, 1)
            dve.wait_ge(route_exp, 1)
            link(nc.vector.tensor_reduce(row_stat[1][:, :], route[1][:, :, :], X_AXIS, ALU.add))
            link(nc.vector.reciprocal(row_stat[2][:, :], row_stat[1][:, :]))
            link(nc.vector.tensor_tensor(route[0][:, :, :], route[1][:, :, :], wide(row_stat[2]), ALU.mult))
            dve.wait_ge(rank_ready, NX)

            def first_largest(p, one_hot):
                link(nc.vector.tensor_reduce(row_stat[3][:, :], p, X_AXIS, ALU.max))
                link(nc.vector.tensor_tensor(route[4][:, :, :], p, wide(row_stat[3]), ALU.is_equal))
                link(nc.vector.tensor_tensor(route[4][:, :, :], route[4][:, :, :], rank_w[:, :, :], ALU.mult))
                link(nc.vector.tensor_reduce(row_stat[4][:, :], route[4][:, :, :], X_AXIS, ALU.max))
                link(nc.vector.tensor_tensor(one_hot, route[4][:, :, :], wide(row_stat[4]), ALU.is_equal))

            first_largest(route[0][:, :, :], route[2][:, :, :])
            link(nc.vector.scalar_tensor_tensor(route[3][:, :, :], route[2][:, :, :], -2.0, route[0][:, :, :], ALU.mult, ALU.add))
            first_largest(route[3][:, :, :], route[5][:, :, :])
            link(nc.vector.tensor_tensor(route[5][:, :, :], route[5][:, :, :], route[2][:, :, :], ALU.add))
            nc.vector.tensor_tensor(gate[:, :, :], route[5][:, :, :], route[0][:, :, :], ALU.mult).then_inc(gate_done, 1)
            dve.wait_ge(gate_done, 1)
            dve.wait_ge(x1_kept, HEAD + B)

            def chunk(c, first):
                nc.vector.tensor_copy(gate_c[:, :, :], gate[:, bass.ds(c * CT, CT), :]).then_inc(gate_staged, 1)
                dve.wait_ge(gate_staged, c + 1)
                for e in range(NX):
                    dve.wait_ge(y_ready, c * NX + (e + 1))
                    if e:
                        dve.wait_ge(y_added, c * (NX * CT) + e * CT)
                    for n in range(CT):
                        base = x1[:, bass.ds(c * CT + n, 1), :].rearrange("p n e -> p (n e)") if e == 0 else acc[:, n, :]
                        nc.vector.scalar_tensor_tensor(acc[:, n, :], y_bank[e % 4][:, n * E:(n + 1) * E], gate_c[:, n, e:e + 1],
                                                       base, ALU.mult, ALU.add).then_inc(y_added, 1)
                dve.wait_ge(y_added, c * (NX * CT) + NX * CT)
                dve.wait_ge(bias_ready, c + 1)
                nc.vector.tensor_tensor(acc[:, :, :], bias_bank[:, :].rearrange("p (n e) -> p n e", n=CT),
                                        acc[:, :, :], ALU.add).then_inc(bias_added, 1)
                dve.wait_ge(bias_added, c + 1)
                for n in range(CT):
                    nc.vector.bn_stats(stats2[:, n, :], acc[:, n, :]).then_inc(stats2_done, 1)
                wait_apart(dve, stats2_done, c * CT + CT, dve_passed)
                for n in range(CT):
                    nc.vector.bn_aggr(moments2[:, n, :], stats2[:, n, :]).then_inc(moments2_done, 1)
                dve.wait_ge(rstd2_done, c + 1)
                if not first:
                    dve.wait_ge(stored, c * 16)
                for n in range(CT):
                    nc.vector.tensor_scalar(y_sb[:, n, :], acc[:, n, :], moments2[:, n, 0:1], rstd2[:, n:n + 1],
                                            ALU.subtract, ALU.mult).then_inc(y_normed, 1)

            chunk(0, True)
            with dve.Fori(1, NCH) as c:
                chunk(c, False)

        @block.tensor
        def _(pe):
            mm = nc.tensor.matmul

            def project_qk(b):
                for a in range(2):
                    last = mm(misc[0][:, a * T:(a + 1) * T], wqkv_sb[:, a * E:(a + 1) * E], x_t_sb[:, bass.ds(b.times(T), T)], start=True, stop=True)
                last.then_inc(qk_projected, 1)

            def project_v(b):
                pe.wait_ge(xt_loaded[b.parity], b.pair * 16 + 16)
                for kt in range(2):
                    last = mm(misc[1][:, kt * E:(kt + 1) * E], xt_sb[b.parity][:, kt * P:(kt + 1) * P], wqkv_sb[:, 2 * E:3 * E], start=True, stop=True)
                last.then_inc(v_projected, 1)

            def scores_first_tile(b, g, in_use):
                q, k = qs[b.parity][g // 2], ks[b.parity][g // 2]
                if g % 2 == 0:
                    pe.wait_ge(stacked[b.parity][g // 2], b.pair * 32 + 32)
                if in_use:
                    pe.wait_ge(maxima, b.times(3 * QUADS, 3 * g - 2))
                mm(score_bank[0][:, :], ident_bf[:, :], mask_first[:, :].unsqueeze(1).to_broadcast([P, 4, P]), start=True, stop=True)
                for i in range(4):
                    h = 4 * (g % 2) + i
                    last = mm(score_bank[0][:, i * P:(i + 1) * P], q[0:ROWS, h, 0:P], k[0:ROWS, h, 0:P], start=False, stop=True, skip_group_check=True)
                last.then_inc(scores_ready, 1)

            def scores_second_tile(b, g, u, in_use):
                q, k = qs[b.parity][g // 2], ks[b.parity][g // 2]
                bank_u = score_bank[1 + u]
                if in_use:
                    pe.wait_ge(maxima, b.times(3 * QUADS, 3 * g - (1 - u)))
                edges = bank_u[:, 0:384].rearrange("p (h a c) -> p h a c", h=2, a=3)[:, :, 0:3:2, :]
                mm(edges, ident_bf[:, :], mask_second[:, :, :].unsqueeze(1).to_broadcast([P, 2, 2, 64]), start=True, stop=True)
                for i in range(2):
                    h = 4 * (g % 2) + 2 * u + i
                    for half in range(2):
                        lo = 64 * half
                        last = mm(bank_u[lo:lo + 64, i * 192:(i + 1) * 192], q[0:ROWS, h, P + lo:P + lo + 64], k[0:ROWS, h, lo:lo + 192],
                                  start=False, stop=True, skip_group_check=True)
                last.then_inc(scores_ready, 1)

            def turned_scores(b, g, i, started):
                q, k = qs[b.parity][g // 2], ks[b.parity][g // 2]
                if g % 2 == 0 and i == 0:
                    pe.wait_ge(max_stacked[b.parity][g // 2], b.pair * 16 + 16)
                n, h = 4 * g + i, 4 * (g % 2) + i
                if started or n >= 2:
                    pe.wait_ge(exp_done, b.times(H, n - 1))
                out_bank = st_bank[n % 2]
                mm(out_bank[:, 0:T], k[0:KROWS, h, 0:P], q[0:KROWS, h, :], start=True, stop=True)
                mm(out_bank[:, T:T + P], k[0:KROWS, h, P:T], q[0:KROWS, h, P:T], start=True, stop=True).then_inc(st_ready, 1)

            def weigh_values(b, g):
                t, s = g // 2, g % 2
                pe.wait_ge(masked, b.times(2 * QUADS, 2 * g + 2))
                if g == 0:
                    pe.wait_ge(v_padded, b.times(4, 4))
                for kt in range(2):
                    for j in range(4):
                        h = 4 * g + j
                        v = v_sb[b.parity][:, kt, h, :]
                        rows = slice(VW * j, VW * (j + 1))
                        if kt == 0:
                            last = mm(o_bank[rows, t * T:(t + 1) * T], v, probs[g][:, 0:2, j, :], start=s == 0, stop=s == 1, skip_group_check=True)
                        else:
                            last = mm(o_bank[rows, t * T + P:(t + 1) * T], v, probs[g][:, 2, j, :], start=False, stop=s == 1, skip_group_check=True)
                last.then_inc(pv_done, 1)

            def turn_max(b, h):
                turned = misc[0][0:PARTS * HALF, :].bitcast(BF16)
                pe.wait_ge(max_split, b.times(2, h + 1))
                for n in range(2):
                    last = nc.tensor.transpose(turned[:, n * P:(n + 1) * P], max_parts[:, n, :, :].rearrange("p a h -> p (a h)"), ident_bf[:, :])
                last.then_inc(max_turned, 1)

            def turn_output(b):
                pe.wait_ge(o_copied, b.times(1, 1))
                for n in range(2):
                    for t in range(2):
                        last = nc.tensor.transpose(misc[1][:, (2 * n + t) * P:(2 * n + t + 1) * P], o_t[:, t, n * P:(n + 1) * P], ident[:, :])
                last.then_inc(o_turned, 1)

            def turn_attention(b):
                pe.wait_ge(normed, b.times(4, 4))
                for n in range(2):
                    last = nc.tensor.transpose(misc[0][:, n * P:(n + 1) * P], attn[:, n, :], ident[:, :])
                last.then_inc(attn_turned, 1)

            def project_out(b):
                pe.wait_ge(attn_copied, b.times(1, 1))
                for n in range(2):
                    last = mm(misc[1][:, n * E:(n + 1) * E], attn_t[:, n * P:(n + 1) * P], wout_sb[:, :], start=True, stop=True)
                last.then_inc(projected, 1)

            def turn_x1(b):
                pe.wait_ge(x1_done, b.times(2, 2))
                for n in range(2):
                    last = nc.tensor.transpose(misc[1][:, n * P:(n + 1) * P], x1_pair[:, n, :], ident[:, :])
                last.then_inc(x1_turned, 1)

            def route_logits(b):
                pe.wait_ge(x1_copied, b.times(1, 1))
                for n in range(2):
                    last = mm(misc[1][:, n * NX:(n + 1) * NX], x1_t[:, n * P:(n + 1) * P], router_sb[:, :], start=True, stop=True)
                last.then_inc(logits_ready, 1)

            for count in (x1_turned, logits_ready):
                pe.sem_inc(count, HEAD)
            pe.wait_ge(qkv_w_loaded, 16)
            pe.wait_ge(x_t_loaded[0], 16)
            project_qk(Batch(0, 0))
            pe.wait_ge(consts_ready, 7)
            pe.wait_ge(ones_ready, 4)

            def step(s, on, n):
                loop = n is None
                before = s.plus(-1), s.plus(-2), s.plus(-3)
                for g in range(QUADS):
                    in_use = loop or n > 0 or g > 0
                    if on["score"]:
                        scores_first_tile(s, g, in_use)
                    if on["prob"]:
                        turned_scores(before[0], g, 0, loop or n > 1)
                    if on["score"]:
                        scores_second_tile(s, g, 0, in_use)
                    if on["prob"]:
                        turned_scores(before[0], g, 1, loop or n > 1)

                    if g == 0 and on["proj"]:
                        if n == 0:
                            pe.wait_ge(part_rest, 1)
                        elif n == 1 or n == 2:
                            pe.wait_ge(max_copied, before[0].times(2, 1))
                        else:
                            pe.wait_ge(attn_copied, before[2].times(1, 1))
                        if n == 1:
                            pe.wait_ge(x_t_loaded[1], 16)
                        project_qk(s.plus(1))
                    if g == 1 and on["score"]:
                        if loop or n >= 3:
                            pe.wait_ge(resid_done, before[2].times(1, 1))
                        elif n >= 1:
                            pe.wait_ge(v_padded, before[0].times(4, 4))
                        project_v(s)
                    if g == 3 and on["tail"]:
                        if on["score"]:
                            pe.wait_ge(max_copied, s.times(2, 1))
                        elif on["prob"]:
                            pe.wait_ge(max_copied, before[0].times(2, 2))
                        else:
                            pe.wait_ge(attn_copied, before[2].times(1, 1))
                        turn_attention(before[1])

                    if on["score"]:
                        scores_second_tile(s, g, 1, in_use)
                    if on["prob"]:
                        turned_scores(before[0], g, 2, loop or n > 1)

                    if g == 2 and on["score"]:
                        if on["prob"]:
                            pe.wait_ge(max_copied, before[0].times(2, 2))
                        else:
                            pe.wait_ge(part_rest, 2)
                        turn_max(s, 0)
                    if g == 3 and on["turn"]:
                        route_logits(before[2])

                    if on["prob"]:
                        turned_scores(before[0], g, 3, loop or n > 1)
                    if g == 0 and on["pv_last"]:
                        weigh_values(before[1], QUADS - 1)
                    if g > 0 and on["prob"]:
                        if g == 1 and (loop or n > 1):
                            pe.wait_ge(o_copied, before[1].times(1, 1))
                        weigh_values(before[0], g - 1)

                    if g == 0 and on["prob"]:
                        if on["proj"]:
                            pe.wait_ge(part_rest, s.plus(1).times(1, 1))
                        else:
                            pe.wait_ge(attn_copied, before[2].times(1, 1))
                        turn_max(before[0], 1)
                    if g == 1 and on["tail"]:
                        if on["score"]:
                            pe.wait_ge(v_padded, s.times(4, 4))
                        else:
                            pe.wait_ge(resid_done, before[2].times(1, 1))
                        turn_output(before[1])
                    if g == 2 and on["turn"]:
                        if on["tail"]:
                            pe.wait_ge(normed, before[1].times(4, 4))
                        else:
                            pe.wait_ge(resid_done, before[2].times(1, 1))
                        turn_x1(before[2])
                    if g == 3 and on["tail"]:
                        if on["turn"]:
                            pe.wait_ge(logits_copied, before[2].times(1, HEAD + 1))
                        else:
                            pe.wait_ge(normed, before[1].times(4, 4))
                        project_out(before[1])
                if n == 1:
                    pe.wait_ge(out_w_loaded, 16)
                    pe.wait_ge(moe_w_loaded, 16 * 5)

            all_steps(pe, step)

            def first_layer(c, e, first):
                if e >= 2 or not first:
                    pe.wait_ge(gelu_done, c * NX + (e - 1))
                cols = bass.ds(c * CH, CH)
                for i, (w, xx) in enumerate(((w_in_lo, x1_hi), (w_in_hi, x1_lo), (w_in_hi, x1_hi))):
                    last = mm(bank[e % 2][:, :], w[:, e, :], xx[:, cols], start=i == 0, stop=i == 2)
                last.then_inc(hid_ready, 1)

            def second_layer(c, e, first):
                pe.wait_ge(gelu_done, c * NX + (e + 1))
                if e >= 4 or not first:
                    pe.wait_ge(y_added, c * (NX * CT) + (e - 3) * CT)
                for n in range(CT):
                    last = mm(y_bank[e % 4][:, n * E:(n + 1) * E], hid[e % 2][:, n * P:(n + 1) * P], w_out_sb[:, e, :], start=True, stop=True)
                last.then_inc(y_ready, 1)

            def chunk(c, first):
                first_layer(c, 0, first)
                for e in range(1, NX):
                    first_layer(c, e, first)
                    if e == GATES_AFTER:
                        pe.wait_ge(gate_staged, c + 1)
                        for n in range(CT):
                            last = nc.tensor.transpose(gate_bank[0:NX, n * P:(n + 1) * P], gate_c[:, n, :], ident[:, :])
                        last.then_inc(gate_turned, 1)
                    second_layer(c, e - 1, first)
                    if e == GATES_AFTER + 1:
                        pe.wait_ge(gate_copied, c + 1)
                        if not first:
                            pe.wait_ge(bias_added, c)
                        for n in range(CT):
                            last = mm(bias_bank[:, n * E:(n + 1) * E], gate_t[:, n * P:(n + 1) * P], b_out_sb[:, :], start=True, stop=True)
                        last.then_inc(bias_ready, 1)
                second_layer(c, NX - 1, first)

            pe.wait_ge(w_lo_done, 1)
            pe.wait_ge(x1_lo_done, HEAD + B)
            chunk(0, True)
            with pe.Fori(1, NCH) as c:
                chunk(c, False)


_OUT = (B, T, E)


def kernel(L0_attn_x, L0_attn_w_qkv, L0_attn_w_out, L0_ffn_router_w, L0_ffn_w_in, L0_ffn_b_in, L0_ffn_w_out, L0_ffn_b_out):
    import numpy as np
    import concourse.bacc as bacc
    from concourse.bass_utils import run_bass_kernel_spmd

    x = np.asarray(L0_attn_x)
    tokens = x.reshape(B * T, E)
    wqkv = np.asarray(L0_attn_w_qkv)
    by_dim = (np.arange(E) % H) * D + np.arange(E) // H
    wq, wk, wv = wqkv[0:E][by_dim], wqkv[E:2 * E][by_dim], wqkv[2 * E:3 * E]
    arrays = {
        "x_t": tokens.T,
        "x": tokens,
        "wqkv_t": np.concatenate([wq, wk, wv], 0).T,
        "wout_t": np.asarray(L0_attn_w_out).T,
        "router_w": np.asarray(L0_ffn_router_w),
        "w_in": np.asarray(L0_ffn_w_in),
        "b_in_t": np.asarray(L0_ffn_b_in).T,
        "w_out": np.asarray(L0_ffn_w_out),
        "b_out": np.asarray(L0_ffn_b_out),
    }
    arrays = {name: np.ascontiguousarray(a) for name, a in arrays.items()}
    nc = bacc.Bacc("TRN2", target_bir_lowering=False, num_devices=1)
    args = [nc.dram_tensor(name, a.shape, F32, kind="ExternalInput").ap() for name, a in arrays.items()]
    args.append(nc.dram_tensor("out", (B * T, E), F32, kind="ExternalOutput").ap())
    attention_moe(nc, *args)
    r = run_bass_kernel_spmd(nc, [arrays], core_ids=[0])
    return r.results[0]["out"].reshape(_OUT)
```

```python
import concourse.bass as bass
from concourse import mybir
from contextlib import ExitStack

F32 = mybir.dt.float32
F32R = mybir.dt.float32r
BF16 = mybir.dt.bfloat16
ALU = mybir.AluOpType
ACT = mybir.ActivationFunctionType
X_AXIS = mybir.AxisListType.X

P = 128
B = 8
T = 256
E = 128
H = 16
D = E // H
W = 128
NX = 8
PARTS = 3
BLK = PARTS * D
ROWS = PARTS * BLK
KROWS = ROWS + PARTS
QUADS = H // 4
HALF = H // 2
TILES = B * T // P
CH = 512
CT = CH // P
NCH = B * T // CH
VW = 32
SCALE = 1.0 / float(D) ** 0.5
EPS = 1e-5
GATES_AFTER = 5
LOAD_WARM_UP = 7
WARM_UP = 34
MASKED = -(2.0 ** 100)
HEAD = 1


class Batch:

    def __init__(self, pair, parity):
        self.pair, self.parity = pair, parity

    def plus(self, k):
        t = self.parity + k
        return Batch(self.pair + t // 2, t % 2)

    def times(self, per, more=0):
        return self.pair * (2 * per) + (per * self.parity + more)


def wait_apart(engine, semaphore, value, passed):
    engine.wait_ge(semaphore, value)
    engine.sem_inc(passed, 1)


def attention_moe(nc, x_t, x, wqkv_t, wout_t, router_w, w_in, b_in_t, w_out, b_out, out):
    q_scratch = nc.dram_tensor("q_scratch", [2 * PARTS * E, T], BF16, kind="Internal").ap()
    k_scratch = nc.dram_tensor("k_scratch", [2 * (2 * PARTS - 1) * E, T], BF16, kind="Internal").ap()

    with ExitStack() as ctx:
        def sb(name, shape, dt=F32):
            return ctx.enter_context(nc.sbuf_tensor(name, shape, dt))

        def sem(name):
            return ctx.enter_context(nc.semaphore(name))

        bank = [ctx.enter_context(nc.psum_tensor(f"bank{i}", [P, 512], F32)) for i in range(8)]
        score_bank, st_bank, o_bank = bank[0:3], bank[3:5], bank[5]
        misc = bank[6:8]
        hid_bank = [bank[2], bank[0]]
        y_bank = [bank[1], bank[3], bank[4], bank[5]]
        gate_bank, bias_bank = bank[6], bank[7]

        ident = sb("ident", [P, P])
        ident_bf = sb("ident_bf", [P, P], BF16)
        mask_first = sb("mask_first", [P, P], BF16)
        mask_second = sb("mask_second", [P, 2, 64], BF16)
        idle_rows = sb("idle_rows", [P, CH], BF16)
        half_power = sb("half_power", [P, CT])
        wqkv_sb = sb("wqkv_sb", [P, 3 * E])
        wout_sb = sb("wout_sb", [P, E])
        router_sb = sb("router_sb", [P, NX])
        b_in_sb = sb("b_in_sb", [P, NX])
        b_out_sb = sb("b_out_sb", [NX, E])
        w_in_sb = sb("w_in_sb", [P, NX, P])
        w_in_hi = sb("w_in_hi", [P, NX, P], F32R)
        w_in_lo = sb("w_in_lo", [P, NX, P], F32R)
        w_out_sb = sb("w_out_sb", [P, NX, E])
        x_t_sb = sb("x_t_sb", [P, B * T])
        xt_sb = [sb(f"x_cols{i}", [P, T]) for i in range(2)]
        x_sb = [sb(f"x_rows{i}", [P, 2, E]) for i in range(2)]
        parts = [sb(f"parts{i}", [P, PARTS, 2, T], BF16) for i in range(2)]
        rest = sb("rest", [P, 2, T])
        qs = [[sb(f"qs{i}{h}", [P, HALF, T], BF16) for h in range(2)] for i in range(2)]
        ks = [[sb(f"ks{i}{h}", [P, HALF, T], BF16) for h in range(2)] for i in range(2)]
        v_sb = [sb(f"v{i}", [P, 2, H, VW]) for i in range(2)]
        neg_max = sb("neg_max", [P, 2, H])
        max_rest = sb("max_rest", [P, 2, HALF])
        max_parts = sb("max_parts", [P, 2, PARTS, HALF], BF16)
        max_t = [sb(f"max_t{h}", [PARTS * HALF, T], BF16) for h in range(2)]
        probs = [sb(f"probs{g}", [P, 3, 4, P]) for g in range(QUADS)]
        o_t = sb("o_t", [P, 2, T])
        inv_sum = sb("inv_sum", [P, 2, H])
        attn = sb("attn", [P, 2, E])
        attn_t = sb("attn_t", [P, T])
        resid = sb("resid", [P, 2, E])
        stats = sb("stats", [P, 2, 6])
        moments = sb("moments", [P, 2, 2])
        var_eps = sb("var_eps", [P, 2])
        rstd = sb("rstd", [P, 2])
        x1 = sb("x1_rows", [P, TILES, E])
        x1_pair = sb("x1_pair", [P, 2, E])
        x1_t = sb("x1_t", [P, T])
        x1_hi = sb("x1_hi", [P, B * T], F32R)
        x1_lo = sb("x1_lo", [P, B * T], F32R)
        logits = sb("logits", [P, TILES, NX])
        route = [sb(f"route{i}", [P, TILES, NX]) for i in range(6)]
        row_stat = [sb(f"row_stat{i}", [P, TILES]) for i in range(6)]
        rank_w = sb("rank_w", [P, TILES, NX])
        gate = sb("gate", [P, TILES, NX])
        gate_c = sb("gate_c", [P, CT, NX])
        gate_t = sb("gate_t", [NX, CH])
        hid = [sb(f"hid{i}", [P, CH]) for i in range(2)]
        stats2 = sb("stats2", [P, CT, 6])
        moments2 = sb("moments2", [P, CT, 2])
        var2 = sb("var2", [P, CT])
        rstd2 = sb("rstd2", [P, CT])
        y_sb = sb("y_sb", [P, CT, E])

        qkv_w_loaded, out_w_loaded, moe_w_loaded = sem("qkv_w_loaded"), sem("out_w_loaded"), sem("moe_w_loaded")
        x_t_loaded = [sem(f"x_t_loaded{i}") for i in range(2)]
        xt_loaded = [sem(f"xt_loaded{i}") for i in range(2)]
        x_loaded = [sem(f"x_loaded{i}") for i in range(2)]
        consts_ready = sem("consts_ready")
        sp_passed, pool_passed, dve_passed = sem("sp_passed"), sem("pool_passed"), sem("dve_passed")
        idle_zeroed = sem("idle_zeroed")
        base_ready, ones_ready = sem("base_ready"), sem("ones_ready")
        v_zeroed, v_ones = sem("v_zeroed"), sem("v_ones")
        maxima, x1_kept = sem("maxima"), sem("x1_kept")
        qk_projected, v_projected = sem("qk_projected"), sem("v_projected")
        part_top, part_rest, part_mid, part_low = sem("part_top"), sem("part_rest"), sem("part_mid"), sem("part_low")
        scratch_written = [sem(f"scratch_written{i}") for i in range(2)]
        stacked = [[sem(f"stacked{i}{h}") for h in range(2)] for i in range(2)]
        v_padded = sem("v_padded")
        scores_ready = sem("scores_ready")
        max_top, max_rested, max_mid, max_split = sem("max_top"), sem("max_rested"), sem("max_mid"), sem("max_split")
        max_turned, max_copied = sem("max_turned"), sem("max_copied")
        max_stacked = [[sem(f"max_stacked{i}{h}") for h in range(2)] for i in range(2)]
        st_ready, exp_done, masked, pv_done = sem("st_ready"), sem("exp_done"), sem("masked"), sem("pv_done")
        o_copied, o_turned, sums_inverted, normed = sem("o_copied"), sem("o_turned"), sem("sums_inverted"), sem("normed")
        attn_turned, attn_copied, projected = sem("attn_turned"), sem("attn_copied"), sem("projected")
        resid_done, stats_done, moments_done = sem("resid_done"), sem("stats_done"), sem("moments_done")
        eps_added, rstd_done, x1_done = sem("eps_added"), sem("rstd_done"), sem("x1_done")
        x1_turned, x1_copied, x1_hi_done, x1_lo_done = sem("x1_turned"), sem("x1_copied"), sem("x1_hi_done"), sem("x1_lo_done")
        logits_ready, logits_copied = sem("logits_ready"), sem("logits_copied")
        w_hi_done, w_lo_done = sem("w_hi_done"), sem("w_lo_done")
        routing, route_shifted, route_exp, gate_done = sem("routing"), sem("route_shifted"), sem("route_exp"), sem("gate_done")
        rank_ready = sem("rank_ready")
        gate_staged, gate_turned, gate_copied, bias_ready = sem("gate_staged"), sem("gate_turned"), sem("gate_copied"), sem("bias_ready")
        hid_ready, gelu_done, y_ready, y_added = sem("hid_ready"), sem("gelu_done"), sem("y_ready"), sem("y_added")
        bias_added, stats2_done, moments2_done = sem("bias_added"), sem("stats2_done"), sem("moments2_done")
        eps2_added, rstd2_done, y_normed = sem("eps2_added"), sem("rstd2_done"), sem("y_normed")
        stored = [sem(f"stored{i}") for i in range(2)]

        block = ctx.enter_context(nc.Block())

        FULL = dict(proj=True, score=True, prob=True, tail=True, turn=True, pv_last=True)
        STEPS_BEFORE = [
            (0, dict(FULL, proj=False, prob=False, tail=False, turn=False, pv_last=False)),
            (1, dict(FULL, tail=False, turn=False, pv_last=False)),
            (2, dict(FULL, turn=False)),
        ]
        LOOP_STEPS = (3, 7)
        STEPS_AFTER = [
            (7, dict(FULL, proj=False)),
            (8, dict(FULL, proj=False, score=False)),
        ]
        LAST = Batch(B // 2 - 1, 1)
        LAST_BUT_1 = Batch(B // 2 - 1, 0)
        EARLY, LATE = slice(0, TILES // 2), slice(TILES // 2, TILES)

        def st_banks(spare):
            return st_bank + score_bank[0:2] if spare else st_bank

        def all_steps(engine, step):
            for s, on in STEPS_BEFORE:
                step(Batch(s // 2, s % 2), on, s)
            with engine.Fori(LOOP_STEPS[0] // 2, LOOP_STEPS[1] // 2) as pair:
                step(Batch(pair, 1), FULL, None)
                step(Batch(pair, 1).plus(1), FULL, None)
            for s, on in STEPS_AFTER:
                step(Batch(s // 2, s % 2), on, s)

        @block.sync
        def _(sp):
            def load_xt(b):
                sp.dma_start(xt_sb[b.parity][:, :], x_t[:, bass.ds(b.times(T), T)]).then_inc(xt_loaded[b.parity], 16)

            def load_x(b):
                sp.dma_start(x_sb[b.parity][:, :, :],
                             x[bass.ds(b.times(T), T), :].rearrange("(n p) e -> p n e", p=P)) \
                    .then_inc(x_loaded[b.parity], 16)

            def write_parts(b):
                par = b.parity
                q0, k0 = par * PARTS * E, par * (2 * PARTS - 1) * E
                sp.wait_ge(part_low, b.times(1, 1))
                sp.dma_start(q_scratch[q0:q0 + PARTS * E, :].rearrange("(a r) t -> r a t", a=PARTS),
                             parts[par][:, :, 0, :]).then_inc(scratch_written[par], 16)
                sp.dma_start(k_scratch[k0:k0 + PARTS * E, :].rearrange("(a r) t -> r a t", a=PARTS),
                             parts[par][:, :, 1, :]).then_inc(scratch_written[par], 16)
                sp.dma_start(k_scratch[k0 + PARTS * E:k0 + (2 * PARTS - 1) * E, :]
                             .rearrange("(a r) t -> r a t", a=PARTS - 1),
                             parts[par][:, 0:PARTS - 1, 1, :]).then_inc(scratch_written[par], 16)

            def stack(b, h, in_use):
                par = b.parity
                if h == 0:
                    wait_apart(sp, scratch_written[par], b.pair * 48 + 48, sp_passed)
                if in_use:
                    sp.wait_ge(st_ready, b.plus(-2).times(H, HALF * (h + 1)))
                for scratch, operand, copies, step_r in ((q_scratch, qs, PARTS, 0), (k_scratch, ks, 2 * PARTS - 1, D * H * T)):
                    at = par * copies * E * T + h * HALF * T
                    sp.dma_start(operand[par][h][0:ROWS, :, :],
                                 bass.AP(scratch.tensor, scratch.offset + at, [[step_r, PARTS], [H * T, BLK], [1, HALF * T]])) \
                        .then_inc(stacked[par][h], 16)

            b0, b1 = Batch(0, 0), Batch(0, 1)

            def stack_max(b, h):
                sp.wait_ge(max_copied, b.times(2, h + 1))
                sp.dma_start(qs[b.parity][h][ROWS:KROWS, :, :], max_t[h][:, :]).then_inc(max_stacked[b.parity][h], 16)

            sp.dma_start(wqkv_sb[:, :], wqkv_t).then_inc(qkv_w_loaded, 16)
            sp.dma_start(x_t_sb[:, 0:2 * T], x_t[:, 0:2 * T]).then_inc(x_t_loaded[0], 16)
            load_xt(b0)
            load_xt(b1)
            sp.dma_start(wout_sb[:, :], wout_t).then_inc(out_w_loaded, 16)
            load_x(b0)
            load_x(b1)
            sp.dma_start(router_sb[:, :], router_w).then_inc(moe_w_loaded, 16)
            sp.dma_start(b_in_sb[:, :], b_in_t).then_inc(moe_w_loaded, 16)
            sp.dma_start(b_out_sb[:, :], b_out).then_inc(moe_w_loaded, 16)
            sp.dma_start(x_t_sb[:, 2 * T:B * T], x_t[:, 2 * T:B * T]).then_inc(x_t_loaded[1], 16)
            sp.wait_ge(ones_ready, 2)
            write_parts(b0)
            write_parts(b1)
            stack(b0, 0, False)
            stack(b0, 1, False)
            sp.wait_ge(ones_ready, 4)
            stack(b1, 0, False)
            stack(b1, 1, False)

            def step(s, on, n):
                if n == 1:
                    sp.dma_start(w_in_sb[:, :, :], w_in.rearrange("e d h -> d e h")).then_inc(moe_w_loaded, 16)
                    sp.dma_start(w_out_sb[:, :, :], w_out.rearrange("e h d -> h e d")).then_inc(moe_w_loaded, 16)
                if n == B:
                    stack_max(s.plus(-1), 1)
                if on["proj"]:
                    write_parts(s.plus(1))
                if n is None or 3 <= n <= B:
                    wait_apart(sp, resid_done, s.plus(-3).times(1, 1), sp_passed)
                    load_x(s.plus(-1))
                if on["proj"]:
                    wait_apart(sp, v_projected, s.plus(-1).times(1, 1), sp_passed)
                    load_xt(s.plus(1))
                    stack(s.plus(1), 0, True)
                if on["score"]:
                    stack_max(s, 0)
                if on["proj"]:
                    stack(s.plus(1), 1, True)

            all_steps(sp, step)
            with sp.Fori(0, NCH) as c:
                for half in range(2):
                    wait_apart(sp, y_normed, c * CT + (2 * half + 2), sp_passed)
                    sp.dma_start(out[bass.ds(c * CH + half * (CH // 2), CH // 2), :].rearrange("(n p) e -> p n e", p=P),
                                 y_sb[:, 2 * half:2 * half + 2, :]).then_inc(stored[half], 16)
            for half in range(2):
                sp.wait_ge(stored[half], NCH * 16)

        @block.gpsimd
        def _(pool):
            pool.sem_inc(x1_kept, HEAD)
            pool.memset(ident[:, :], 0.0).then_inc(base_ready, 1)
            pool.memset(ident_bf[:, :], 0.0).then_inc(base_ready, 1)
            pool.memset(mask_first[:, :], 0.0).then_inc(base_ready, 1)
            pool.memset(mask_second[:, :, :], 0.0).then_inc(base_ready, 1)
            pool.memset(half_power[:, :], -0.5).then_inc(base_ready, 1)
            pool.wait_ge(base_ready, 5)
            for m in (ident, ident_bf):
                pool.affine_select(out=m[:, :], in_=m[:, :], compare_op=ALU.not_equal, fill=1.0, base=0,
                                   pattern=[[-1, P]], channel_multiplier=1).then_inc(consts_ready, 1)
            pool.affine_select(out=mask_first[:, :], in_=mask_first[:, :], compare_op=ALU.is_ge, fill=MASKED, base=0,
                               pattern=[[-1, P]], channel_multiplier=1).then_inc(consts_ready, 1)
            for lo in (0, 64):
                pool.wait_ge(consts_ready, 3 + lo // 32)
                part = mask_second[lo:lo + 64, 0, :]
                pool.affine_select(out=part, in_=part, compare_op=ALU.is_gt, fill=MASKED, base=0,
                                   pattern=[[1, 64]], channel_multiplier=-1).then_inc(consts_ready, 1)
                part = mask_second[lo:lo + 64, 1, :]
                pool.affine_select(out=part, in_=part, compare_op=ALU.is_ge, fill=MASKED, base=0,
                                   pattern=[[-1, 64]], channel_multiplier=1).then_inc(consts_ready, 1)
            pool.wait_ge(consts_ready, 7)
            for par in range(2):
                pool.memset(v_sb[par][:, :, :, :], 0.0).then_inc(v_zeroed, 1)
            pool.wait_ge(v_zeroed, 2)
            for par in range(2):
                for kt in range(2):
                    for s in range(2):
                        ones = v_sb[par][:, kt, :, :].rearrange("p (t s j) c -> p t s j c", t=2, s=2)[:, :, s, :, (D + 1) * s + D]
                        pool.memset(ones, 1.0).then_inc(v_ones, 1)
            for e in range(NX):
                pool.memset(rank_w[:, :, e:e + 1], float(NX - e)).then_inc(rank_ready, 1)

            def first_deviation(b):
                wait_apart(pool, moments_done, b.times(2, 2), pool_passed)
                pool.tensor_scalar(var_eps[:, :], moments[:, :, 1], EPS, None, ALU.add).then_inc(eps_added, 1)
                pool.wait_ge(eps_added, b.times(1, 1))
                pool.tensor_tensor(rstd[:, :], var_eps[:, :], half_power[:, 0:2], ALU.pow).then_inc(rstd_done, 1)

            def keep_x1(b):
                pool.wait_ge(x1_done, b.times(2, 2))
                pool.tensor_copy(x1[:, bass.ds(b.times(2), 2), :], x1_pair[:, :, :]).then_inc(x1_kept, 1)

            def step(s, on, n):
                if on["turn"]:
                    first_deviation(s.plus(-3))
                for g in range(QUADS):
                    if on["prob"]:
                        b = s.plus(-1)
                        wait_apart(pool, exp_done, b.times(H, 4 * g + 4), pool_passed)
                        own, other = probs[g][:, 0:3:2, :, :], probs[g][:, 1, :, :]
                        pool.affine_select(out=own, in_=own, compare_op=ALU.is_ge,
                                           fill=0.0, base=0, pattern=[[0, 2], [0, 4], [1, P]],
                                           channel_multiplier=-1).then_inc(masked, 1)
                        pool.affine_select(out=other, in_=other, compare_op=ALU.is_gt,
                                           fill=0.0, base=0, pattern=[[0, 4], [-1, P]],
                                           channel_multiplier=1).then_inc(masked, 1)
                    if g == 1 and on["turn"]:
                        keep_x1(s.plus(-3))

            all_steps(pool, step)
            for b in (LAST_BUT_1, LAST):
                first_deviation(b)
                keep_x1(b)
            with pool.Fori(0, NCH) as c:
                for half in range(2):
                    two = slice(2 * half, 2 * half + 2)
                    wait_apart(pool, moments2_done, c * CT + (2 * half + 2), pool_passed)
                    pool.tensor_scalar(var2[:, two], moments2[:, two, 1], EPS, None, ALU.add).then_inc(eps2_added, 1)
                    pool.wait_ge(eps2_added, c * 2 + (half + 1))
                    pool.tensor_tensor(rstd2[:, two], var2[:, two], half_power[:, two], ALU.pow).then_inc(rstd2_done, 1)

        @block.scalar
        def _(act):
            def exponentials(b, g, i, in_use, spare):
                k = 4 * g + i
                if i == 0 and in_use:
                    act.wait_ge(pv_done, b.plus(-1).times(QUADS, g + 1))
                act.wait_ge(st_ready, b.times(H, k + 1))
                nc.scalar.activation(probs[g][:, :, i, :], st_banks(spare)[k % len(st_banks(spare))][:, 0:3 * P].rearrange("p (k c) -> p k c", k=3), ACT.Exp, scale=SCALE) \
                    .then_inc(exp_done, 1)

            def copy_max(b, h, in_use):
                act.wait_ge(max_turned, b.times(2, h + 1))
                if in_use:
                    act.wait_ge(max_stacked[b.plus(-1).parity][h], b.plus(-1).pair * 16 + 16)
                nc.scalar.activation(max_t[h][:, :], misc[0][0:PARTS * HALF, :].bitcast(BF16)[:, 0:T], ACT.Copy).then_inc(max_copied, 1)

            def copy_output(b, in_use):
                act.wait_ge(pv_done, b.times(QUADS, QUADS))
                if in_use:
                    act.wait_ge(o_turned, b.plus(-1).times(1, 1))
                nc.scalar.activation(o_t[:, :, :], o_bank[:, :].rearrange("p (t q) -> p t q", t=2), ACT.Copy).then_inc(o_copied, 1)

            def copy_attention(b, in_use):
                act.wait_ge(attn_turned, b.times(1, 1))
                if in_use:
                    act.wait_ge(projected, b.plus(-1).times(1, 1))
                nc.scalar.activation(attn_t[:, :], misc[0][:, 0:T], ACT.Copy).then_inc(attn_copied, 1)

            def copy_x1(b, in_use):
                act.wait_ge(x1_turned, b.times(1, HEAD + 1))
                if in_use:
                    act.wait_ge(x1_lo_done, b.times(1, HEAD))
                    act.wait_ge(logits_ready, b.times(1, HEAD))
                nc.scalar.activation(x1_t[:, :], misc[1][:, 0:T], ACT.Copy).then_inc(x1_copied, 1)

            def copy_logits(b):
                act.wait_ge(logits_ready, b.times(1, HEAD + 1))
                nc.scalar.activation(logits[:, bass.ds(b.times(2), 2), :],
                                     misc[1][:, 0:2 * NX].rearrange("p (n e) -> p n e", n=2), ACT.Copy).then_inc(logits_copied, 1)

            def route_exponentials(tiles, k):
                act.wait_ge(route_shifted, k)
                nc.scalar.activation(route[1][:, tiles, :], route[0][:, tiles, :], ACT.Exp).then_inc(route_exp, 1)

            def stack_second_max(b):
                act.wait_ge(max_copied, b.times(2, 2))
                act.dma_start(qs[b.parity][1][ROWS:KROWS, :, :], max_t[1][:, :]).then_inc(max_stacked[b.parity][1], 16)

            def step(s, on, n):
                if n == B:
                    copy_max(s.plus(-1), 1, True)
                for g in range(QUADS):
                    for i in range(4):
                        if on["prob"]:
                            exponentials(s.plus(-1), g, i, n is None or n >= 2, n == B)
                        if (g, i) == (0, 1) and on["proj"]:
                            take_top(s.plus(1), n is None or n >= 1)
                        if (g, i) == (1, 0) and on["prob"] and on["score"]:
                            stack_second_max(s.plus(-1))
                        if (g, i) == (1, 1) and on["score"]:
                            pad_v(s, n is None or n >= 2)
                        if (g, i) == (3, 1) and on["tail"]:
                            copy_attention(s.plus(-2), n is None or n >= 3)
                        if (g, i) == (2, 2) and on["score"]:
                            copy_max(s, 0, n is None or n >= 1)
                        if (g, i) == (3, 2) and on["turn"]:
                            copy_logits(s.plus(-3))
                    if g == 0 and on["pv_last"]:
                        copy_output(s.plus(-2), n is None or n >= 3)
                    if g == 0 and on["prob"] and on["score"]:
                        copy_max(s.plus(-1), 1, n is None or n >= 2)
                    if g == 2 and on["turn"]:
                        copy_x1(s.plus(-3), n is None or n >= 4)
                    if g == 1 and n == B:
                        route_exponentials(EARLY, 1)

            def take_top(b, in_use):
                act.wait_ge(qk_projected, b.times(1, 1))
                if in_use:
                    act.wait_ge(scratch_written[b.parity], b.plus(-2).pair * 48 + 48)
                nc.scalar.activation(parts[b.parity][:, 0, :, :], misc[0][:, :].rearrange("p (a t) -> p a t", a=2), ACT.Copy).then_inc(part_top, 1)

            def pad_v(b, in_use):
                act.wait_ge(v_projected, b.times(1, 1))
                if in_use:
                    act.wait_ge(pv_done, b.plus(-2).times(QUADS, QUADS))
                else:
                    act.wait_ge(v_ones, 8)
                for kt in range(2):
                    for s in range(2):
                        dst = v_sb[b.parity][:, kt, :, (D + 1) * s:(D + 1) * s + D].rearrange("p (t s j) c -> p t s j c", t=2, s=2)[:, :, s, :, :]
                        src = misc[1][:, kt * E:(kt + 1) * E].rearrange("p (t s j c) -> p t s j c", t=2, s=2, j=4)[:, :, s, :, :]
                        nc.scalar.activation(dst, src, ACT.Copy).then_inc(v_padded, 1)

            act.sem_inc(logits_copied, HEAD)
            take_top(Batch(0, 0), False)
            take_top(Batch(0, 1), False)
            all_steps(act, step)

            def gelu(c, e, first):
                act.wait_ge(hid_ready, c * NX + (e + 1))
                if e >= 2 or not first:
                    act.wait_ge(y_ready, c * NX + (e - 1))
                nc.scalar.activation(hid[e % 2][:, :], hid_bank[e % 2][:, :], ACT.Gelu_apprx_tanh,
                                     bias=b_in_sb[:, e:e + 1]).then_inc(gelu_done, 1)
                if e == GATES_AFTER:
                    act.wait_ge(gate_turned, c + 1)
                    nc.scalar.activation(gate_t[:, :], gate_bank[0:NX, :], ACT.Copy).then_inc(gate_copied, 1)

            gelu(0, 0, True)
            gelu(0, 1, True)
            copy_output(LAST, True)
            gelu(0, 2, True)
            copy_attention(LAST, True)
            copy_x1(LAST_BUT_1, True)
            gelu(0, 3, True)
            copy_logits(LAST_BUT_1)
            gelu(0, 4, True)
            gelu(0, 5, True)
            copy_x1(LAST, True)
            gelu(0, 6, True)
            copy_logits(LAST)
            route_exponentials(LATE, 2)
            gelu(0, 7, True)
            with act.Fori(1, NCH) as c:
                for e in range(NX):
                    gelu(c, e, False)

        @block.vector
        def _(dve):
            links = 0

            def link(ins):
                nonlocal links
                links += 1
                ins.then_inc(routing, 1)
                dve.wait_ge(routing, links)

            def route_shift(tiles, last, k):
                wide = row_stat[0][:, tiles].unsqueeze(2).to_broadcast([P, TILES // 2, NX])
                dve.wait_ge(logits_copied, last.times(1, HEAD + 1))
                link(nc.vector.tensor_reduce(row_stat[0][:, tiles], logits[:, tiles, :], X_AXIS, ALU.max))
                nc.vector.tensor_tensor(route[0][:, tiles, :], logits[:, tiles, :], wide, ALU.subtract).then_inc(route_shifted, 1)

            def choose(tiles, k):
                def wide(ap):
                    return ap[:, tiles].unsqueeze(2).to_broadcast([P, TILES // 2, NX])

                def first_largest(p, one_hot):
                    r4 = route[4][:, tiles, :]
                    link(nc.vector.tensor_reduce(row_stat[3][:, tiles], p, X_AXIS, ALU.max))
                    link(nc.vector.tensor_tensor(r4, p, wide(row_stat[3]), ALU.is_equal))
                    link(nc.vector.tensor_tensor(r4, r4, rank_w[:, tiles, :], ALU.mult))
                    link(nc.vector.tensor_reduce(row_stat[4][:, tiles], r4, X_AXIS, ALU.max))
                    link(nc.vector.tensor_tensor(one_hot, r4, wide(row_stat[4]), ALU.is_equal))

                prob, first, rest_p, second = (route[i][:, tiles, :] for i in (0, 2, 3, 5))
                dve.wait_ge(route_exp, k)
                dve.wait_ge(rank_ready, NX)
                link(nc.vector.tensor_reduce(row_stat[1][:, tiles], route[1][:, tiles, :], X_AXIS, ALU.add))
                link(nc.vector.reciprocal(row_stat[2][:, tiles], row_stat[1][:, tiles]))
                link(nc.vector.tensor_tensor(prob, route[1][:, tiles, :], wide(row_stat[2]), ALU.mult))
                first_largest(prob, first)
                link(nc.vector.scalar_tensor_tensor(rest_p, first, -2.0, prob, ALU.mult, ALU.add))
                first_largest(rest_p, second)
                link(nc.vector.tensor_tensor(second, second, first, ALU.add))
                nc.vector.tensor_tensor(gate[:, tiles, :], second, prob, ALU.mult).then_inc(gate_done, 1)
                dve.wait_ge(gate_done, k)

            def split_rest(b, in_use=True):
                p = parts[b.parity]
                dve.wait_ge(part_top, b.times(1, 1))
                if in_use:
                    dve.wait_ge(part_low, b.times(1))
                nc.vector.tensor_tensor(rest[:, :, :], misc[0][:, :].rearrange("p (a t) -> p a t", a=2), p[:, 0, :, :],
                                        ALU.subtract).then_inc(part_rest, 1)
                dve.wait_ge(part_rest, b.times(1, 1))
                nc.vector.tensor_copy(p[:, 1, :, :], rest[:, :, :]).then_inc(part_mid, 1)
                dve.wait_ge(part_mid, b.times(1, 1))
                nc.vector.tensor_tensor(p[:, 2, :, :], rest[:, :, :], p[:, 1, :, :], ALU.subtract).then_inc(part_low, 1)

            def split_max(b, h, in_use):
                full = neg_max[:, :, h * HALF:(h + 1) * HALF]
                k = b.times(2, h + 1)
                dve.wait_ge(maxima, b.times(3 * QUADS, 3 * (QUADS // 2) * (h + 1)))
                if in_use:
                    dve.wait_ge(max_turned, b.times(2, h))
                nc.vector.tensor_copy(max_parts[:, :, 0, :], full).then_inc(max_top, 1)
                dve.wait_ge(max_top, k)
                nc.vector.tensor_tensor(max_rest[:, :, :], full, max_parts[:, :, 0, :], ALU.subtract).then_inc(max_rested, 1)
                dve.wait_ge(max_rested, k)
                nc.vector.tensor_copy(max_parts[:, :, 1, :], max_rest[:, :, :]).then_inc(max_mid, 1)
                dve.wait_ge(max_mid, k)
                nc.vector.tensor_tensor(max_parts[:, :, 2, :], max_rest[:, :, :], max_parts[:, :, 1, :], ALU.subtract).then_inc(max_split, 1)

            def normalise(b):
                turned = misc[1][:, :].rearrange("p (n t j c) -> p n t j c", n=2, t=2, j=4)
                dve.wait_ge(o_turned, b.times(1, 1))
                for n in range(2):
                    nc.vector.reciprocal(inv_sum[:, n, :].rearrange("p (t s j) -> p t j s", t=2, s=2),
                                         turned[:, n, :, :, D:2 * (D + 1):D + 1]).then_inc(sums_inverted, 1)
                dve.wait_ge(sums_inverted, b.times(2, 2))
                for n in range(2):
                    for t in range(2):
                        src = turned[:, n, t, :, 0:2 * (D + 1)].rearrange("p j (s c) -> p s j c", s=2)[:, :, :, 0:D]
                        inv = inv_sum[:, n, t * HALF:(t + 1) * HALF].rearrange("p (s j) -> p s j", s=2).unsqueeze(3).to_broadcast([P, 2, 4, D])
                        dst = attn[:, n, t * 64:(t + 1) * 64].rearrange("p (s j c) -> p s j c", s=2, j=4)
                        nc.vector.tensor_tensor(dst, src, inv, ALU.mult).then_inc(normed, 1)

            def first_residual(b):
                dve.wait_ge(projected, b.times(1, 1))
                dve.wait_ge(x_loaded[b.parity], b.pair * 16 + 16)
                nc.vector.tensor_tensor(resid[:, :, :], misc[1][:, 0:T].rearrange("p (n e) -> p n e", n=2),
                                        x_sb[b.parity][:, :, :], ALU.add).then_inc(resid_done, 1)

            def first_stats(b):
                dve.wait_ge(resid_done, b.times(1, 1))
                for n in range(2):
                    nc.vector.bn_stats(stats[:, n, :], resid[:, n, :]).then_inc(stats_done, 1)

            def first_moments(b):
                wait_apart(dve, stats_done, b.times(2, 2), dve_passed)
                for n in range(2):
                    nc.vector.bn_aggr(moments[:, n, :], stats[:, n, :]).then_inc(moments_done, 1)

            def first_norm(b, in_use):
                dve.wait_ge(rstd_done, b.times(1, 1))
                if in_use:
                    dve.wait_ge(x1_kept, b.times(1, HEAD))
                    dve.wait_ge(x1_turned, b.times(1, HEAD))
                for n in range(2):
                    nc.vector.tensor_scalar(x1_pair[:, n, :], resid[:, n, :], moments[:, n, 0:1], rstd[:, n:n + 1],
                                            ALU.subtract, ALU.mult).then_inc(x1_done, 1)

            def split_x1(b):
                cols = bass.ds(b.times(T), T)
                dve.wait_ge(x1_copied, b.times(1, 1))
                nc.vector.tensor_copy(x1_hi[:, cols], x1_t[:, :]).then_inc(x1_hi_done, 1)
                dve.wait_ge(x1_hi_done, b.times(1, 1))
                nc.vector.tensor_tensor(x1_lo[:, cols], x1_t[:, :], x1_hi[:, cols].bitcast(F32), ALU.subtract).then_inc(x1_lo_done, 1)

            def max_first_tile(s, g):
                dve.wait_ge(scores_ready, s.times(3 * QUADS, 3 * g + 1))
                nc.vector.tensor_reduce(neg_max[:, 0, 4 * g:4 * g + 4], score_bank[0][:, :].rearrange("p (h c) -> p h c", h=4),
                                        X_AXIS, ALU.max, negate=True).then_inc(maxima, 1)

            def max_second_tile(s, g, u):
                dve.wait_ge(scores_ready, s.times(3 * QUADS, 3 * g + 2 + u))
                nc.vector.tensor_reduce(neg_max[:, 1, 4 * g + 2 * u:4 * g + 2 * u + 2],
                                        score_bank[1 + u][:, 0:384].rearrange("p (h c) -> p h c", h=2),
                                        X_AXIS, ALU.max, negate=True).then_inc(maxima, 1)

            def step(s, on, n):
                for g in range(QUADS):
                    if g == 0 and on["turn"]:
                        first_residual(s.plus(-3))
                    if g == 1 and on["turn"]:
                        first_norm(s.plus(-3), n is None or n >= 4)
                    if on["score"]:
                        if g == 0 and (n is None or n >= 1):
                            dve.wait_ge(max_split, s.plus(-1).times(2, 2))
                        max_first_tile(s, g)
                    if g == 0 and on["turn"]:
                        first_stats(s.plus(-3))
                    if g == 2 and on["tail"]:
                        normalise(s.plus(-2))
                    if g == 3 and on["turn"]:
                        split_x1(s.plus(-3))
                    if g == 0 and n == B:
                        route_shift(EARLY, Batch(B // 4, 0), 1)
                    if g == 3 and n == B:
                        choose(EARLY, 1)
                    if on["score"]:
                        max_second_tile(s, g, 0)
                    if g == 0 and on["turn"]:
                        first_moments(s.plus(-3))
                    if g == 0 and on["proj"]:
                        split_rest(s.plus(1))
                    if on["score"]:
                        max_second_tile(s, g, 1)
                        if g == 1:
                            split_max(s, 0, n is None or n >= 1)
                        if g == 3:
                            split_max(s, 1, True)
                if n == 1:
                    dve.wait_ge(moe_w_loaded, 16 * 5)
                    nc.vector.tensor_copy(w_in_hi[:, :, :], w_in_sb[:, :, :]).then_inc(w_hi_done, 1)
                    dve.wait_ge(w_hi_done, 1)
                    nc.vector.tensor_tensor(w_in_lo[:, :, :], w_in_sb[:, :, :], w_in_hi[:, :, :].bitcast(F32), ALU.subtract).then_inc(w_lo_done, 1)

            dve.sem_inc(x1_lo_done, HEAD)
            nc.vector.memset(idle_rows[:, :], 0.0).then_inc(idle_zeroed, 1)
            def ones_below(par):
                for h in range(2):
                    nc.vector.memset(ks[par][h][64:P, :, :], 1.0).then_inc(ones_ready, 1)

            ones_below(0)
            split_rest(Batch(0, 0), False)
            split_rest(Batch(0, 1), True)
            ones_below(1)
            all_steps(dve, step)

            def stage_gates(c):
                nc.vector.tensor_copy(gate_c[:, :, :], gate[:, bass.ds(c * CT, CT), :]).then_inc(gate_staged, 1)
                dve.wait_ge(gate_staged, c + 1)

            def token_rows(c, n):
                return x1[:, bass.ds(c * CT + n, 1), :].rearrange("p n e -> p (n e)")

            def add_expert(c, e):
                dve.wait_ge(y_ready, c * NX + (e + 1))
                for n in range(CT):
                    if e == NX - 1:
                        if n == 0:
                            dve.wait_ge(bias_added, c + 1)
                    elif e:
                        dve.wait_ge(y_added, c * (NX * CT) + ((e - 1) * CT + n + 1))
                    nc.vector.scalar_tensor_tensor(token_rows(c, n), y_bank[e % 4][:, n * E:(n + 1) * E], gate_c[:, n, e:e + 1],
                                                   token_rows(c, n), ALU.mult, ALU.add).then_inc(y_added, 1)

            def add_bias(c):
                dve.wait_ge(bias_ready, c + 1)
                dve.wait_ge(y_added, c * (NX * CT) + (NX - 1) * CT)
                rows = x1[:, bass.ds(c * CT, CT), :]
                nc.vector.tensor_tensor(rows, bias_bank[:, :].rearrange("p (n e) -> p n e", n=CT), rows, ALU.add).then_inc(bias_added, 1)

            def second_stats(c, half):
                wait_apart(dve, y_added, c * (NX * CT) + ((NX - 1) * CT + 2 * half + 2), dve_passed)
                for n in (2 * half, 2 * half + 1):
                    nc.vector.bn_stats(stats2[:, n, :], token_rows(c, n)).then_inc(stats2_done, 1)

            def second_moments(c, half):
                wait_apart(dve, stats2_done, c * CT + 2 * half + 2, dve_passed)
                for n in (2 * half, 2 * half + 1):
                    nc.vector.bn_aggr(moments2[:, n, :], stats2[:, n, :]).then_inc(moments2_done, 1)

            def second_norm(c, half, first):
                dve.wait_ge(rstd2_done, c * 2 + (half + 1))
                if not first:
                    dve.wait_ge(stored[half], c * 16)
                for n in (2 * half, 2 * half + 1):
                    nc.vector.tensor_scalar(y_sb[:, n, :], token_rows(c, n), moments2[:, n, 0:1], rstd2[:, n:n + 1],
                                            ALU.subtract, ALU.mult).then_inc(y_normed, 1)

            def second_statistics(c):
                second_stats(c, 0)
                second_stats(c, 1)
                second_moments(c, 0)
                second_moments(c, 1)

            first_residual(LAST_BUT_1)
            first_stats(LAST_BUT_1)
            first_moments(LAST_BUT_1)
            stage_gates(0)
            normalise(LAST)
            first_norm(LAST_BUT_1, True)
            add_expert(0, 0)
            split_x1(LAST_BUT_1)
            add_expert(0, 1)
            first_residual(LAST)
            first_stats(LAST)
            first_moments(LAST)
            add_expert(0, 2)
            first_norm(LAST, True)
            add_expert(0, 3)
            add_expert(0, 4)
            split_x1(LAST)
            add_expert(0, 5)
            route_shift(LATE, LAST, 2)
            add_expert(0, 6)
            add_bias(0)
            add_expert(0, 7)
            second_statistics(0)

            def chunk(c, norm_before, routing=()):
                stage_gates(c)
                add_expert(c, 0)
                norm_before()
                for e in range(1, NX - 1):
                    add_expert(c, e)
                    if e == 2 and routing:
                        choose(*routing)
                add_bias(c)
                add_expert(c, NX - 1)
                second_statistics(c)

            def norm(c, first):
                second_norm(c, 0, first)
                second_norm(c, 1, first)

            chunk(1, lambda: norm(0, True), (LATE, 2))
            dve.wait_ge(x1_kept, HEAD + B)
            with dve.Fori(2, NCH) as c:
                chunk(c, lambda: norm(c - 1, False))
            norm(NCH - 1, False)

        @block.tensor
        def _(pe):
            mm = nc.tensor.matmul

            def project_qk(b):
                for a in range(2):
                    last = mm(misc[0][:, a * T:(a + 1) * T], wqkv_sb[:, a * E:(a + 1) * E], x_t_sb[:, bass.ds(b.times(T), T)], start=True, stop=True)
                last.then_inc(qk_projected, 1)

            def project_v(b):
                pe.wait_ge(xt_loaded[b.parity], b.pair * 16 + 16)
                for kt in range(2):
                    last = mm(misc[1][:, kt * E:(kt + 1) * E], xt_sb[b.parity][:, kt * P:(kt + 1) * P], wqkv_sb[:, 2 * E:3 * E], start=True, stop=True)
                last.then_inc(v_projected, 1)

            def scores_first_tile(b, g, in_use):
                q, k = qs[b.parity][g // 2], ks[b.parity][g // 2]
                if g % 2 == 0:
                    pe.wait_ge(stacked[b.parity][g // 2], b.pair * 32 + 32)
                if in_use:
                    pe.wait_ge(maxima, b.times(3 * QUADS, 3 * g - 2))
                mm(score_bank[0][:, :], ident_bf[:, :], mask_first[:, :].unsqueeze(1).to_broadcast([P, 4, P]), start=True, stop=True)
                for i in range(4):
                    h = 4 * (g % 2) + i
                    last = mm(score_bank[0][:, i * P:(i + 1) * P], q[0:ROWS, h, 0:P], k[0:ROWS, h, 0:P], start=False, stop=True, skip_group_check=True)
                last.then_inc(scores_ready, 1)

            def scores_second_tile(b, g, u, in_use):
                q, k = qs[b.parity][g // 2], ks[b.parity][g // 2]
                bank_u = score_bank[1 + u]
                if in_use:
                    pe.wait_ge(maxima, b.times(3 * QUADS, 3 * g - (1 - u)))
                edges = bank_u[:, 0:384].rearrange("p (h a c) -> p h a c", h=2, a=3)[:, :, 0:3:2, :]
                mm(edges, ident_bf[:, :], mask_second[:, :, :].unsqueeze(1).to_broadcast([P, 2, 2, 64]), start=True, stop=True)
                for i in range(2):
                    h = 4 * (g % 2) + 2 * u + i
                    for half in range(2):
                        lo = 64 * half
                        last = mm(bank_u[lo:lo + 64, i * 192:(i + 1) * 192], q[0:ROWS, h, P + lo:P + lo + 64], k[0:ROWS, h, lo:lo + 192],
                                  start=False, stop=True, skip_group_check=True)
                last.then_inc(scores_ready, 1)

            def turned_scores(b, g, i, started, spare=False):
                q, k = qs[b.parity][g // 2], ks[b.parity][g // 2]
                if g % 2 == 0 and i == 0:
                    pe.wait_ge(max_stacked[b.parity][g // 2], b.pair * 16 + 16)
                n, h = 4 * g + i, 4 * (g % 2) + i
                if spare and n >= 4:
                    pe.wait_ge(exp_done, b.times(H, n - 3))
                elif spare and n >= 2:
                    pe.wait_ge(maxima, b.times(3 * QUADS, 3 * QUADS))
                elif started or n >= 2:
                    pe.wait_ge(exp_done, b.times(H, n - 1))
                out_bank = st_banks(spare)[n % len(st_banks(spare))]
                mm(out_bank[:, 0:T], k[0:KROWS, h, 0:P], q[0:KROWS, h, :], start=True, stop=True)
                mm(out_bank[:, T:T + P], k[0:KROWS, h, P:T], q[0:KROWS, h, P:T], start=True, stop=True).then_inc(st_ready, 1)

            def weigh_values(b, g):
                t, s = g // 2, g % 2
                pe.wait_ge(masked, b.times(2 * QUADS, 2 * g + 2))
                if g == 0:
                    pe.wait_ge(v_padded, b.times(4, 4))
                for kt in range(2):
                    for j in range(4):
                        h = 4 * g + j
                        v = v_sb[b.parity][:, kt, h, :]
                        rows = slice(VW * j, VW * (j + 1))
                        if kt == 0:
                            last = mm(o_bank[rows, t * T:(t + 1) * T], v, probs[g][:, 0:2, j, :], start=s == 0, stop=s == 1, skip_group_check=True)
                        else:
                            last = mm(o_bank[rows, t * T + P:(t + 1) * T], v, probs[g][:, 2, j, :], start=False, stop=s == 1, skip_group_check=True)
                last.then_inc(pv_done, 1)

            def turn_max(b, h):
                turned = misc[0][0:PARTS * HALF, :].bitcast(BF16)
                pe.wait_ge(max_split, b.times(2, h + 1))
                for n in range(2):
                    last = nc.tensor.transpose(turned[:, n * P:(n + 1) * P], max_parts[:, n, :, :].rearrange("p a h -> p (a h)"), ident_bf[:, :])
                last.then_inc(max_turned, 1)

            def turn_output(b):
                pe.wait_ge(o_copied, b.times(1, 1))
                for n in range(2):
                    for t in range(2):
                        last = nc.tensor.transpose(misc[1][:, (2 * n + t) * P:(2 * n + t + 1) * P], o_t[:, t, n * P:(n + 1) * P], ident[:, :])
                last.then_inc(o_turned, 1)

            def turn_attention(b):
                pe.wait_ge(normed, b.times(4, 4))
                for n in range(2):
                    last = nc.tensor.transpose(misc[0][:, n * P:(n + 1) * P], attn[:, n, :], ident[:, :])
                last.then_inc(attn_turned, 1)

            def project_out(b):
                pe.wait_ge(attn_copied, b.times(1, 1))
                for n in range(2):
                    last = mm(misc[1][:, n * E:(n + 1) * E], attn_t[:, n * P:(n + 1) * P], wout_sb[:, :], start=True, stop=True)
                last.then_inc(projected, 1)

            def turn_x1(b):
                pe.wait_ge(x1_done, b.times(2, 2))
                for n in range(2):
                    last = nc.tensor.transpose(misc[1][:, n * P:(n + 1) * P], x1_pair[:, n, :], ident[:, :])
                last.then_inc(x1_turned, 1)

            def route_logits(b):
                pe.wait_ge(x1_copied, b.times(1, 1))
                for n in range(2):
                    last = mm(misc[1][:, n * NX:(n + 1) * NX], x1_t[:, n * P:(n + 1) * P], router_sb[:, :], start=True, stop=True)
                last.then_inc(logits_ready, 1)

            def first_layer(c, e, first):
                if e >= 2 or not first:
                    pe.wait_ge(gelu_done, c * NX + (e - 1))
                elif e == 1:
                    pe.wait_ge(exp_done, B * H - 1)
                cols = bass.ds(c * CH, CH)
                for i, (w, xx) in enumerate(((w_in_lo, x1_hi), (w_in_hi, x1_lo), (w_in_hi, x1_hi))):
                    last = mm(hid_bank[e % 2][:, :], w[:, e, :], xx[:, cols], start=i == 0, stop=i == 2)
                last.then_inc(hid_ready, 1)

            def second_layer(c, e, first):
                pe.wait_ge(gelu_done, c * NX + (e + 1))
                if e >= 4 or not first:
                    pe.wait_ge(y_added, c * (NX * CT) + (e - 3) * CT)
                for n in range(CT):
                    last = mm(y_bank[e % 4][:, n * E:(n + 1) * E], hid[e % 2][:, n * P:(n + 1) * P], w_out_sb[:, e, :], start=True, stop=True)
                last.then_inc(y_ready, 1)

            def unit(c, e, first):
                first_layer(c, e, first)
                if e == GATES_AFTER:
                    pe.wait_ge(gate_staged, c + 1)
                    for n in range(CT):
                        last = nc.tensor.transpose(gate_bank[0:NX, n * P:(n + 1) * P], gate_c[:, n, :], ident[:, :])
                    last.then_inc(gate_turned, 1)
                if e:
                    second_layer(c, e - 1, first)

            def finish(c, first, more=True):
                pe.wait_ge(gate_copied, c + 1)
                if not first:
                    pe.wait_ge(bias_added, c)
                for n in range(CT):
                    last = mm(bias_bank[:, n * E:(n + 1) * E], gate_t[:, n * P:(n + 1) * P], b_out_sb[:, :], start=True, stop=True)
                last.then_inc(bias_ready, 1)
                if more:
                    first_layer(c + 1, 0, False)
                second_layer(c, NX - 1, first)

            def keep_warm(count):
                for _ in range(count):
                    mm(o_bank[:, :], idle_rows[:, 0:P], idle_rows[:, :], start=True, stop=True)

            for count in (x1_turned, logits_ready):
                pe.sem_inc(count, HEAD)
            pe.wait_ge(idle_zeroed, 1)
            keep_warm(LOAD_WARM_UP)
            pe.wait_ge(qkv_w_loaded, 16)
            pe.wait_ge(x_t_loaded[0], 16)
            project_qk(Batch(0, 0))
            pe.wait_ge(part_rest, 1)
            project_qk(Batch(0, 1))
            pe.wait_ge(consts_ready, 7)
            keep_warm(WARM_UP)

            def step(s, on, n):
                loop = n is None
                before = s.plus(-1), s.plus(-2), s.plus(-3)
                for g in range(QUADS):
                    in_use = loop or n > 0 or g > 0
                    if g == 0 and n == B:
                        pe.wait_ge(attn_copied, before[2].times(1, 1))
                        turn_max(before[0], 1)
                    if on["score"]:
                        scores_first_tile(s, g, in_use)
                    if n == 1 and g == 0:
                        keep_warm(4)
                    if on["prob"]:
                        turned_scores(before[0], g, 0, loop or n > 1, n == B)
                    if on["score"]:
                        scores_second_tile(s, g, 0, in_use)
                    if on["prob"]:
                        turned_scores(before[0], g, 1, loop or n > 1, n == B)

                    if g == 0 and on["proj"]:
                        if n == 1 or n == 2:
                            pe.wait_ge(max_copied, before[0].times(2, 1))
                        else:
                            pe.wait_ge(attn_copied, before[2].times(1, 1))
                        if n == 1:
                            pe.wait_ge(x_t_loaded[1], 16)
                        project_qk(s.plus(1))
                    if g == 1 and on["score"]:
                        if loop or n >= 3:
                            pe.wait_ge(resid_done, before[2].times(1, 1))
                        elif n >= 1:
                            pe.wait_ge(v_padded, before[0].times(4, 4))
                        project_v(s)
                    if g == 3 and on["tail"]:
                        if on["score"]:
                            pe.wait_ge(max_copied, s.times(2, 1))
                        elif on["prob"]:
                            pe.wait_ge(max_copied, before[0].times(2, 2))
                        else:
                            pe.wait_ge(attn_copied, before[2].times(1, 1))
                        turn_attention(before[1])

                    if on["score"]:
                        scores_second_tile(s, g, 1, in_use)
                    if on["prob"]:
                        turned_scores(before[0], g, 2, loop or n > 1, n == B)

                    if g >= 2 and n == 0:
                        keep_warm(2)
                    if g == 2 and on["score"]:
                        if on["prob"]:
                            pe.wait_ge(max_copied, before[0].times(2, 2))
                        else:
                            pe.wait_ge(part_rest, 2)
                        turn_max(s, 0)
                    if g == 3 and on["turn"]:
                        route_logits(before[2])
                    if g == 3 and n == B:
                        pe.wait_ge(w_lo_done, 1)
                        unit(0, 0, True)

                    if on["prob"]:
                        turned_scores(before[0], g, 3, loop or n > 1, n == B)
                    if g == 0 and on["pv_last"]:
                        weigh_values(before[1], QUADS - 1)
                    lag = 2 if n == B else 1
                    if g >= lag and on["prob"]:
                        if g == lag and (loop or n > 1):
                            pe.wait_ge(o_copied, before[1].times(1, 1))
                        weigh_values(before[0], g - lag)

                    if g == 0 and n == 1:
                        keep_warm(3)
                    if g == 0 and on["prob"] and on["score"]:
                        if on["proj"]:
                            pe.wait_ge(part_rest, s.plus(1).times(1, 1))
                        else:
                            pe.wait_ge(attn_copied, before[2].times(1, 1))
                        turn_max(before[0], 1)
                    if g == 1 and on["tail"]:
                        if on["score"]:
                            pe.wait_ge(v_padded, s.times(4, 4))
                        else:
                            pe.wait_ge(resid_done, before[2].times(1, 1))
                        turn_output(before[1])
                    if g == 2 and on["turn"]:
                        if on["tail"]:
                            pe.wait_ge(normed, before[1].times(4, 4))
                        else:
                            pe.wait_ge(resid_done, before[2].times(1, 1))
                        turn_x1(before[2])
                    if g == 3 and on["tail"]:
                        if on["turn"]:
                            pe.wait_ge(logits_copied, before[2].times(1, HEAD + 1))
                        else:
                            pe.wait_ge(normed, before[1].times(4, 4))
                        project_out(before[1])
                if n == 1:
                    pe.wait_ge(out_w_loaded, 16)
                    pe.wait_ge(moe_w_loaded, 16 * 5)

            all_steps(pe, step)

            weigh_values(LAST, QUADS - 2)
            first_layer(0, 1, True)
            weigh_values(LAST, QUADS - 1)
            second_layer(0, 0, True)
            pe.wait_ge(resid_done, LAST_BUT_1.times(1, 1))
            turn_output(LAST)
            unit(0, 2, True)
            turn_attention(LAST)
            turn_x1(LAST_BUT_1)
            unit(0, 3, True)
            route_logits(LAST_BUT_1)
            pe.wait_ge(logits_copied, LAST_BUT_1.times(1, HEAD + 1))
            project_out(LAST)
            unit(0, 4, True)
            unit(0, 5, True)
            pe.wait_ge(resid_done, LAST.times(1, 1))
            turn_x1(LAST)
            unit(0, 6, True)
            route_logits(LAST)
            unit(0, 7, True)
            pe.wait_ge(logits_copied, LAST.times(1, HEAD + 1))
            pe.wait_ge(x1_lo_done, HEAD + B)
            finish(0, True)
            with pe.Fori(1, NCH - 1) as c:
                for e in range(1, NX):
                    unit(c, e, False)
                finish(c, False)
            for e in range(1, NX):
                unit(NCH - 1, e, False)
            finish(NCH - 1, False, more=False)


_OUT = (B, T, E)


def kernel(L0_attn_x, L0_attn_w_qkv, L0_attn_w_out, L0_ffn_router_w, L0_ffn_w_in, L0_ffn_b_in, L0_ffn_w_out, L0_ffn_b_out):
    import numpy as np
    import concourse.bacc as bacc
    from concourse.bass_utils import run_bass_kernel_spmd

    x = np.asarray(L0_attn_x)
    tokens = x.reshape(B * T, E)
    wqkv = np.asarray(L0_attn_w_qkv)
    by_dim = (np.arange(E) % H) * D + np.arange(E) // H
    wq, wk, wv = wqkv[0:E][by_dim], wqkv[E:2 * E][by_dim], wqkv[2 * E:3 * E]
    arrays = {
        "x_t": tokens.T,
        "x": tokens,
        "wqkv_t": np.concatenate([wq, wk, wv], 0).T,
        "wout_t": np.asarray(L0_attn_w_out).T,
        "router_w": np.asarray(L0_ffn_router_w),
        "w_in": np.asarray(L0_ffn_w_in),
        "b_in_t": np.asarray(L0_ffn_b_in).T,
        "w_out": np.asarray(L0_ffn_w_out),
        "b_out": np.asarray(L0_ffn_b_out),
    }
    arrays = {name: np.ascontiguousarray(a) for name, a in arrays.items()}
    nc = bacc.Bacc("TRN2", target_bir_lowering=False, num_devices=1)
    args = [nc.dram_tensor(name, a.shape, F32, kind="ExternalInput").ap() for name, a in arrays.items()]
    args.append(nc.dram_tensor("out", (B * T, E), F32, kind="ExternalOutput").ap())
    attention_moe(nc, *args)
    r = run_bass_kernel_spmd(nc, [arrays], core_ids=[0])
    return r.results[0]["out"].reshape(_OUT)
```
